# Optimizing a Trainium2 kernel written in Bass

```python
import numpy as np
import jax
import jax.numpy as jnp

def _softmax(x, axis=-1):
    return jax.nn.softmax(x, axis=axis)

def _gelu(x):
    return jax.nn.gelu(x, approximate=True)

def _silu(x):
    return jax.nn.silu(x)

def _sigmoid(x):
    return jax.nn.sigmoid(x)

def _layernorm(x, axis=-1, eps=1e-05):
    m = jnp.mean(x, axis=axis, keepdims=True)
    v = jnp.var(x, axis=axis, keepdims=True)
    return (x - m) / jnp.sqrt(v + eps)

def _scatter_add(tgt, idx, src, axis=0):
    return tgt.at[idx].add(src)

def _segment_sum(src, seg, n):
    return jax.ops.segment_sum(src, seg, n)
kernel_name = 'mk_adj_preln_d2_adj_r2_ab0a6e'

def setup_inputs(seed: int=0):
    np.random.seed(seed)
    _w = jnp.asarray

    def _rec_inputs():
        import jax
        import jax.numpy as jnp
        _gk = jax.random.key(seed)
        x = -0.0005207 + 1.001 * jax.random.normal(jax.random.fold_in(_gk, 1), (2048, 128), jnp.float32)
        _a = jax.random.bernoulli(jax.random.fold_in(_gk, 2), 0.000976562, (2048, 2048))
        _a = jnp.logical_or(_a, jnp.swapaxes(_a, -1, -2))
        _a = jnp.logical_or(_a, jnp.eye(2048, dtype=bool))
        _af = _a.astype(jnp.float32)
        _af = _af * jax.random.uniform(jax.random.fold_in(_gk, 3), (2048, 2048), jnp.float32, 0.05, 2.05)
        adj = _af
        return (x, adj)
    x, adj = _rec_inputs()

    def _L0_gnn_setup():
        import jax, jax.numpy as jnp
        import numpy as np
        N = 4096
        D = 128
        CUTOFF = 1.0
        MU = 1.0
        SIGMA = 0.5

        def sensitivity(r, mu, sigma):
            return jnp.exp(-(1.0 / r - 1.0 / mu) ** 2 / (2.0 * sigma * sigma))
        key = jax.random.key(seed)
        k_z, k_d, k_w = jax.random.split(key, 3)
        z = jax.random.normal(k_z, (N, D), dtype=jnp.float32)
        dist_matrix = jax.random.uniform(k_d, (N, N), dtype=jnp.float32) * 2.0 + 0.05
        W = jax.random.normal(k_w, (D, D), dtype=jnp.float32)
        B = jnp.zeros((D,), dtype=jnp.float32)
        return {'z': z, 'dist_matrix': dist_matrix, 'W': W, 'B': B}
    _L0_gnn_all = _L0_gnn_setup()
    _L0_gnn_in = {k: v for k, v in _L0_gnn_all.items() if k in ('W', 'B')}
    del _L0_gnn_all

    def _L1_gnn_setup():
        import jax, jax.numpy as jnp
        import numpy as np
        N, H, HEADS = (2048, 128, 3)
        ALPHA = 0.2
        NEG_INF = -9000000000000000.0

        def _sign_adj(key, n, density):
            k1, k2 = jax.random.split(key)
            mask = jax.random.uniform(k1, (n, n)) < density
            sign = jnp.where(jax.random.uniform(k2, (n, n)) < 0.5, -1.0, 1.0)
            adj = jnp.where(mask, sign, 0.0).astype(jnp.float32)
            idx = jnp.arange(n)
            return adj.at[idx, idx].set(1.0)

        def _gru_cell(x, hstate, Wih, Whh, bih, bhh):
            gi = x @ Wih.T + bih
            gh = hstate @ Whh.T + bhh
            ir, iz, inn = jnp.split(gi, 3, axis=1)
            hr, hz, hn = jnp.split(gh, 3, axis=1)
            r = jax.nn.sigmoid(ir + hr)
            z = jax.nn.sigmoid(iz + hz)
            n = jnp.tanh(inn + r * hn)
            return (1.0 - z) * n + z * hstate

        def _gat_head(h, node_adj, edge_adj, W, a):
            hW = h @ W
            hp = (node_adj > 0).astype(hW.dtype) @ hW
            hm = (node_adj < 0).astype(hW.dtype) @ hW
            e_plus = jax.nn.leaky_relu(jnp.concatenate([hp, hm], axis=1) @ a, ALPHA)[:, 0]
            e_minus = jax.nn.leaky_relu(jnp.concatenate([hm, hp], axis=1) @ a, ALPHA)[:, 0]
            att = jnp.where(edge_adj > 0, e_plus[None, :], NEG_INF)
            att = jnp.where(edge_adj < 0, e_minus[None, :], att)
            att = jax.nn.softmax(att, axis=1)
            return att * edge_adj @ hW
        key = jax.random.key(seed)
        ks = jax.random.split(key, 16)
        std = 0.01
        gain = 1.414
        return {'h': jax.random.normal(ks[0], (N, H), jnp.float32), 'node_adj': _sign_adj(ks[1], N, 0.005), 'edge_adj': _sign_adj(ks[2], N, 0.005), 'gat_W': jax.random.normal(ks[3], (HEADS, H, H), jnp.float32) * (gain / np.sqrt(H, dtype=np.float32)), 'gat_a': jax.random.normal(ks[4], (HEADS, 2 * H, 1), jnp.float32) * 0.1, 'edge_Wih': jax.random.normal(ks[5], (3 * H, H), jnp.float32) * std, 'edge_Whh': jax.random.normal(ks[6], (3 * H, H), jnp.float32) * std, 'edge_bih': jnp.zeros((3 * H,), jnp.float32), 'edge_bhh': jnp.zeros((3 * H,), jnp.float32), 'node_Wih': jax.random.normal(ks[7], (3 * H, H), jnp.float32) * std, 'node_Whh': jax.random.normal(ks[8], (3 * H, H), jnp.float32) * std, 'node_bih': jnp.zeros((3 * H,), jnp.float32), 'node_bhh': jnp.zeros((3 * H,), jnp.float32)}
    _L1_gnn_all = _L1_gnn_setup()
    _L1_gnn_in = {k: v for k, v in _L1_gnn_all.items() if k in ('gat_W', 'gat_a', 'edge_Wih', 'edge_Whh', 'edge_bih', 'edge_bhh', 'node_Wih', 'node_Whh', 'node_bih', 'node_bhh')}
    del _L1_gnn_all
    return {'x': x, 'adj': adj, 'L0_gnn_W': _L0_gnn_in['W'], 'L0_gnn_B': _L0_gnn_in['B'], 'L1_gnn_gat_W': _L1_gnn_in['gat_W'], 'L1_gnn_gat_a': _L1_gnn_in['gat_a'], 'L1_gnn_edge_Wih': _L1_gnn_in['edge_Wih'], 'L1_gnn_edge_Whh': _L1_gnn_in['edge_Whh'], 'L1_gnn_edge_bih': _L1_gnn_in['edge_bih'], 'L1_gnn_edge_bhh': _L1_gnn_in['edge_bhh'], 'L1_gnn_node_Wih': _L1_gnn_in['node_Wih'], 'L1_gnn_node_Whh': _L1_gnn_in['node_Whh'], 'L1_gnn_node_bih': _L1_gnn_in['node_bih'], 'L1_gnn_node_bhh': _L1_gnn_in['node_bhh']}

def reference(x, adj, L0_gnn_W, L0_gnn_B, L1_gnn_gat_W, L1_gnn_gat_a, L1_gnn_edge_Wih, L1_gnn_edge_Whh, L1_gnn_edge_bih, L1_gnn_edge_bhh, L1_gnn_node_Wih, L1_gnn_node_Whh, L1_gnn_node_bih, L1_gnn_node_bhh):
    import jax
    import jax.numpy as jnp

    def _L0_gnn_ref(z, dist_matrix, W, B):
        import jax, jax.numpy as jnp
        import numpy as np
        N = 4096
        D = 128
        CUTOFF = 1.0
        MU = 1.0
        SIGMA = 0.5

        def sensitivity(r, mu, sigma):
            return jnp.exp(-(1.0 / r - 1.0 / mu) ** 2 / (2.0 * sigma * sigma))
        msg = z @ W + B
        sens = sensitivity(dist_matrix, MU, SIGMA)
        weights = jnp.where(dist_matrix < CUTOFF, sens, 0.0)
        return weights @ msg

    def _L1_gnn_ref(h, node_adj, edge_adj, gat_W, gat_a, edge_Wih, edge_Whh, edge_bih, edge_bhh, node_Wih, node_Whh, node_bih, node_bhh):
        import jax, jax.numpy as jnp
        import numpy as np
        N, H, HEADS = (2048, 128, 3)
        ALPHA = 0.2
        NEG_INF = -9000000000000000.0

        def _sign_adj(key, n, density):
            k1, k2 = jax.random.split(key)
            mask = jax.random.uniform(k1, (n, n)) < density
            sign = jnp.where(jax.random.uniform(k2, (n, n)) < 0.5, -1.0, 1.0)
            adj = jnp.where(mask, sign, 0.0).astype(jnp.float32)
            idx = jnp.arange(n)
            return adj.at[idx, idx].set(1.0)

        def _gru_cell(x, hstate, Wih, Whh, bih, bhh):
            gi = x @ Wih.T + bih
            gh = hstate @ Whh.T + bhh
            ir, iz, inn = jnp.split(gi, 3, axis=1)
            hr, hz, hn = jnp.split(gh, 3, axis=1)
            r = jax.nn.sigmoid(ir + hr)
            z = jax.nn.sigmoid(iz + hz)
            n = jnp.tanh(inn + r * hn)
            return (1.0 - z) * n + z * hstate

        def _gat_head(h, node_adj, edge_adj, W, a):
            hW = h @ W
            hp = (node_adj > 0).astype(hW.dtype) @ hW
            hm = (node_adj < 0).astype(hW.dtype) @ hW
            e_plus = jax.nn.leaky_relu(jnp.concatenate([hp, hm], axis=1) @ a, ALPHA)[:, 0]
            e_minus = jax.nn.leaky_relu(jnp.concatenate([hm, hp], axis=1) @ a, ALPHA)[:, 0]
            att = jnp.where(edge_adj > 0, e_plus[None, :], NEG_INF)
            att = jnp.where(edge_adj < 0, e_minus[None, :], att)
            att = jax.nn.softmax(att, axis=1)
            return att * edge_adj @ hW
        dn = jnp.diag(node_adj)
        de = jnp.diag(edge_adj)
        idx = jnp.arange(node_adj.shape[0])
        node_adj_norm = node_adj.at[idx, idx].add(-dn)
        edge_adj_norm = edge_adj.at[idx, idx].add(-de)
        node_support = node_adj_norm @ h
        edge_output = _gru_cell(node_support, h, edge_Wih, edge_Whh, edge_bih, edge_bhh)
        edge_support = _gat_head(h, node_adj_norm, edge_adj_norm, gat_W[0], gat_a[0])
        for i in range(1, HEADS):
            edge_support = edge_support + _gat_head(h, node_adj_norm, edge_adj_norm, gat_W[i], gat_a[i])
        edge_support = edge_support / HEADS
        node_output = _gru_cell(edge_support, h, node_Wih, node_Whh, node_bih, node_bhh)
        return de[:, None] * edge_output + dn[:, None] * node_output
    h = jnp.maximum(_layernorm(x, axis=-1), 0.0)
    x = x + _L0_gnn_ref(h, adj, L0_gnn_W, L0_gnn_B)
    h = jnp.maximum(_layernorm(x, axis=-1), 0.0)
    x = x + _L1_gnn_ref(h, adj, adj, L1_gnn_gat_W, L1_gnn_gat_a, L1_gnn_edge_Wih, L1_gnn_edge_Whh, L1_gnn_edge_bih, L1_gnn_edge_bhh, L1_gnn_node_Wih, L1_gnn_node_Whh, L1_gnn_node_bih, L1_gnn_node_bhh)
    return x

_drawn_inputs = setup_inputs


def setup_inputs(seed=0):
    import zlib

    import numpy as np

    out = dict(_drawn_inputs(seed))
    spreads = {'L0_gnn_B': (0.0, 0.537),
     'L1_gnn_edge_bih': (0.0, 0.8),
     'L1_gnn_edge_bhh': (0.0, 2.0),
     'L1_gnn_node_bih': (0.0, 0.8),
     'L1_gnn_node_bhh': (0.0, 2.0)}
    factors = {'L1_gnn_gat_W': 8.0,
     'L1_gnn_gat_a': 8.0,
     'L1_gnn_edge_Wih': 2.825,
     'L1_gnn_edge_Whh': 8.0,
     'L1_gnn_node_Wih': 8.0,
     'L1_gnn_node_Whh': 23.005}
    for name, (base, spread) in spreads.items():
        noise = np.random.default_rng([zlib.crc32(name.encode()), seed]).standard_normal(out[name].shape)
        drawn = base * np.exp(spread * noise) if base else spread * noise
        out[name] = jnp.asarray(drawn.astype(out[name].dtype))
    for name, factor in factors.items():
        out[name] = (out[name] * factor).astype(out[name].dtype)
    return out
```

```python
import math
from contextlib import ExitStack

import numpy as np
import concourse.bass as bass
from concourse import mybir

F32 = mybir.dt.float32
BF16 = mybir.dt.bfloat16
F8 = mybir.dt.float8e5
I32 = mybir.dt.int32
ALU = mybir.AluOpType
ACT = mybir.ActivationFunctionType
AX = mybir.AxisListType

N, D, H, P = 2048, 128, 3, 128
NT = N // P
BLK = 512
NB = N // BLK
KT = BLK // P
NG = 3 * D
HWC = H * D + 2 * H
HC = 3 * H + 1
EPS = 1e-5
TINY = 2.0 ** -60
HUGE = 2.0 ** 127
C = 17.375
OUT = 2.0 ** 100


def program(nc, x, adj, w0, b0, gat_w, gat_a, e_wih, e_whh, e_bih, e_bhh,
            n_wih, n_whh, n_bih, n_bhh, out):
    ctx = ExitStack()
    with ctx:
        def sb(name, shape, dt=F32):
            return ctx.enter_context(nc.sbuf_tensor(name, shape, dt))

        def sem(name):
            return ctx.enter_context(nc.semaphore(name))

        xb = sb("xb", [P, NT, D])
        h2 = sb("h2", [P, NT, D])
        h2t = sb("h2t", [P, N])
        hw = sb("hw", [P, NT, HWC])
        col = sb("col", [P, NB, KT, BLK])
        row = sb("row", [P, 2, N])
        pen = sb("pen", [P, 2, N], BF16)
        sc = sb("sc", [P, 2, N])
        ident = sb("ident", [P, P])
        nident = sb("nident", [P, P])
        ones = sb("ones", [P, P])
        offdiag = sb("offdiag", [P, P], BF16)
        wcat = sb("wcat", [P, HWC])
        w0s = sb("w0s", [P, D])
        b0s = sb("b0s", [P, D])
        gas = sb("gas", [P, H, 2])
        de = sb("de", [P, NT])
        wt = sb("wt", [P, 4, NG])
        bi = sb("bi", [P, 4, 3])
        gb = sb("gb", [P, 2, 2])
        stat = sb("stat", [P, NT, 6])
        mv = sb("mv", [P, NT, 2])
        var = sb("var", [P, NT])
        rstd = sb("rstd", [P, NT])
        nwt = sb("nwt", [P, NT])
        hu3 = sb("hu3", [P, NT, HC], BF16)
        hur = sb("hur", [P, 2, NT, H])
        ew = sb("ew", [P, H, NT])
        qs = sb("qs", [P, NT, H])
        negm = sb("negm", [P, KT * H])
        den = sb("den", [P, KT * H])
        negmc = sb("negmc", [P, KT * H])
        nml = sb("nml", [P, KT * H])
        okc = sb("okc", [P, 2, NT])
        okm = sb("okm", [P, 4])
        flag = sb("flag", [1, 1], I32)
        unused = sb("unused", [1, 16])
        epsb = sb("epsb", [P, 1])
        tinyb = sb("tinyb", [P, 1])
        two = sb("two", [P, 1])

        arena = sb("arena", [P, 18688])

        def part(start, *dims):
            size = int(np.prod(dims))
            view = arena[:, start:start + size]
            if len(dims) == 2:
                view = view.rearrange("p (a b) -> p a b", a=dims[0])
            if len(dims) == 3:
                view = view.rearrange("p (a b c) -> p a b c", a=dims[0], b=dims[1])
            return view

        mask = part(0, NT * N // 4).bitcast(F8).rearrange("p (a b) -> p a b", a=NT)
        rec = part(8192, 4, BLK)
        wgt = part(10240, 4, BLK)
        msg = part(12288, NT, D)
        mstage = part(15872, BLK).bitcast(F8).rearrange("p (a b) -> p a b", a=4)
        xs = part(14336, BLK)
        zr = part(14848, KT, D)
        zt = part(15360, BLK)
        stage = part(14336, 3 * P)
        graw = sc[:, 0, 0:4 * NG].rearrange("p (c g d) -> p c g d", c=4, g=3)

        neb = part(0, H, N)
        nmb = part(6144, H, BLK)
        tt = part(7680, 4, BLK)
        uu = part(9728, 4, BLK)
        att = part(11776, 2, BLK)
        dg = part(12800, 2, H, P)
        gru = part(13568, 9, BLK)
        osb = part(18176, KT, D)
        NSB, ESB, TR, TZ, UV, NN, DD, OE, ST = range(9)

        ps = ctx.enter_context(nc.psum_tensor("ps", [P, 8, 512], F32))

        x_in = sem("x_in")
        weights_in = sem("weights_in")
        gru_w_in = sem("gru_w_in")
        diag_in = sem("diag_in")
        col_in = [sem(f"col_in{s}") for s in range(NB)]
        row_in = [sem(f"row_in{s}") for s in range(2)]
        stored = sem("stored")
        const_set = sem("const_set")
        wprep = sem("wprep")
        wcopied = sem("wcopied")
        p_stat = sem("p_stat")
        recip_ln0 = sem("recip_ln0")
        p_rstd = sem("p_rstd")
        p_z = sem("p_z")
        p_zt = sem("p_zt")
        p_ztc = sem("p_ztc")
        p_msg = sem("p_msg")
        p_msgc = sem("p_msgc")
        vp = sem("vp")
        adj_t = sem("adj_t")
        ln_adj = sem("ln_adj")
        recip = sem("recip")
        mask_done = sem("mask_done")
        mask_kept = sem("mask_kept")
        sq_done = sem("sq_done")
        sens = sem("sens")
        wgt_done = sem("wgt_done")
        summed = sem("summed")
        f_xs = sem("f_xs")
        f_xt = sem("f_xt")
        f_stat = sem("f_stat")
        f_ln = sem("f_ln")
        f_rstd = sem("f_rstd")
        f_z = sem("f_z")
        f_zt = sem("f_zt")
        f_ztc = sem("f_ztc")
        f_keep = sem("f_keep")
        f_hw = sem("f_hw")
        f_hwa = sem("f_hwa")
        f_hwv = sem("f_hwv")
        vf = sem("vf")
        no_self = sem("no_self")
        hu_split = sem("hu_split")
        vt = sem("vt")
        q_done = sem("q_done")
        e_done = sem("e_done")
        e_diag = sem("e_diag")
        e_row = sem("e_row")
        e_rowa = sem("e_rowa")
        e_rowv = sem("e_rowv")
        ok_min = sem("ok_min")
        ok_t = sem("ok_t")
        flag_set = sem("flag_set")
        clean = sem("clean")
        pen_raw = sem("pen_raw")
        pen_done = sem("pen_done")
        max_done = sem("max_done")
        sc_done = sem("sc_done")
        den_done = sem("den_done")
        ln_done = sem("ln_done")
        nml_done = sem("nml_done")
        dg_done = sem("dg_done")
        bc_done = sem("bc_done")
        nmb_done = sem("nmb_done")
        att_t = sem("att_t")
        att_done = sem("att_done")
        t_done = sem("t_done")
        u_done = sem("u_done")
        ns_mm = sem("ns_mm")
        es_mm = sem("es_mm")
        sup_out = sem("sup_out")
        g_mm = sem("g_mm")
        g_act = sem("g_act")
        g_dve = sem("g_dve")
        vg = sem("vg")
        o_sum = sem("o_sum")
        o_t = sem("o_t")
        o_done = sem("o_done")

        adj_cols = adj.rearrange("(b k p) (q c) -> b q p k c", k=KT, p=P, q=NB)
        adj_rows = adj.rearrange("(t p) n -> t p n", p=P)
        out_blocks = out.rearrange("(b k p) d -> b p k d", k=KT, p=P)

        CELL = 3
        OWN = 2 * CELL

        block = ctx.enter_context(nc.Block())

        @block.sync
        def _(sp):
            sp.sem_inc(stored, 16)
            sp.dma_start(xb[:, :, :], x.rearrange("(t p) d -> p t d", p=P)).then_inc(x_in, 16)
            for q in range(NB):
                sp.dma_start(col[:, q, :, :], adj_cols[0, q]).then_inc(col_in[q], 16)
            with nc.sync.Fori(1, NB) as b:
                for q in range(NB):
                    sp.wait_ge(adj_t, NT * b - NT + KT * q + KT)
                    sp.dma_start(col[:, q, :, :], adj_cols[bass.ds(b, 1), q, :, :, :]
                                 .rearrange("o p k c -> (o p) k c")).then_inc(col_in[q], 16)
            for q in range(NB):
                sp.wait_ge(adj_t, NT * (NB - 1) + KT * q + KT)
                sp.dma_start(col[:, q, :, :], adj_cols[0, q]).then_inc(col_in[q], 16)
            def next_block(b, first):
                for q in range(NB):
                    if q == NB - 1 and not first:
                        store(b - 1)
                    sp.wait_ge(att_t, NT * b + KT * q + KT)
                    sp.dma_start(col[:, q, :, :], adj_cols[bass.ds(b + 1, 1), q, :, :, :]
                                 .rearrange("o p k c -> (o p) k c")).then_inc(col_in[q], 16)

            def store(f):
                sp.wait_ge(o_done, f + 1)
                sp.dma_start(out_blocks[bass.ds(f, 1), :, :, :].rearrange("o p k d -> (o p) k d"),
                             osb).then_inc(stored, 16)

            next_block(0, True)
            with nc.sync.Fori(1, NB - 1) as b:
                next_block(b, False)
            store(NB - 2)
            store(NB - 1)
            sp.wait_ge(stored, 16 * NB + 16)

        @block.gpsimd
        def _(pool):
            pool.memset(ident[:, :], 0.0).then_inc(const_set, 1)
            pool.memset(ones[:, :], 1.0).then_inc(const_set, 1)
            pool.memset(epsb[:, :], EPS).then_inc(const_set, 1)
            pool.memset(tinyb[:, :], TINY).then_inc(const_set, 1)
            pool.memset(two[:, :], -2.0).then_inc(const_set, 1)
            pool.memset(hu3[:, :, :], 1.0).then_inc(const_set, 1)
            pool.wait_ge(const_set, 6)
            pool.affine_select(out=ident[:, :], in_=ident[:, :], compare_op=ALU.not_equal, fill=1.0,
                               base=0, pattern=[[-1, P]], channel_multiplier=1).then_inc(const_set, 1)
            pool.wait_ge(const_set, 7)
            pool.tensor_scalar(nident[:, :], ident[:, :], -1.0, 0.0, ALU.mult, ALU.add).then_inc(const_set, 1)
            pool.tensor_scalar(offdiag[:, :], ident[:, :], -1.0, 1.0, ALU.mult, ALU.add).then_inc(const_set, 1)

            pool.dma_start(w0s[:, :], w0).then_inc(weights_in, 16)
            pool.dma_start(b0s[:, :], b0.rearrange("(o d) -> o d", o=1).broadcast_to([P, D])).then_inc(weights_in, 16)
            pool.dma_start(wcat[:, 0:H * D].rearrange("p (h d) -> p h d", h=H),
                           gat_w.rearrange("h p d -> p h d")).then_inc(weights_in, 16)
            pool.dma_start(gas[:, :, :], gat_a.rearrange("h (s p) o -> p h (s o)", s=2),
                           allow_slow_non_contiguous=True).then_inc(weights_in, 16)
            pool.dma_start(de[:, :], bass.AP(adj.tensor, 0, [[N + 1, P], [P * (N + 1), NT], [1, 1]])
                           .rearrange("p t o -> p (t o)"), allow_slow_non_contiguous=True).then_inc(diag_in, 16)
            for c, b_ in enumerate((e_bih, e_bhh, n_bih, n_bhh)):
                pool.dma_start(bi[:, c, :], b_.rearrange("(g p) -> p g", p=P),
                               allow_slow_non_contiguous=True).then_inc(diag_in, 16)

            for c, w in enumerate((e_wih, e_whh, n_wih, n_whh)):
                pool.dma_start(graw[:, c, :, :], w.rearrange("(g p) d -> p g d", p=P)).then_inc(gru_w_in, 16)
            pool.sem_inc(f_keep, 2)

            def keep_h2(f):
                pool.wait_ge(f_z, f + 1)
                pool.tensor_copy(h2[:, bass.ts(f, KT), :], zr).then_inc(f_keep, 1)

            def keep_h2t(f):
                pool.wait_ge(f_ztc, f + 1)
                pool.tensor_copy(h2t[:, bass.ts(f, BLK)], zt).then_inc(f_keep, 1)

            def layer0(b, first):
                for j in range(NT):
                    pool.wait_ge(mask_done, NT * b + j + 1)
                    pool.tensor_copy(mask[:, j, bass.ts(b, BLK)].bitcast(I32), mstage[:, j % 4, :].bitcast(I32))\
                        .then_inc(mask_kept, 1)
                    if not first and j == 8:
                        keep_h2(b - 1)
                    if not first and j == 10:
                        keep_h2t(b - 1)

            layer0(0, True)
            with nc.gpsimd.Fori(1, NB) as b:
                layer0(b, False)
            for t in range(2):
                pool.dma_start(row[:, t, :], adj_rows[t]).then_inc(row_in[t], 16)
            pool.wait_ge(mask_kept, NT * NB)
            for t in range(NT):
                spot = mask[:, t, P * t:P * t + P]
                pool.tensor_tensor(spot, spot, offdiag[:, :], ALU.mult, saturate=False).then_inc(no_self, 1)
            keep_h2(NB - 1)
            keep_h2t(NB - 1)

            def pen_of(t):
                pool.wait_ge(row_in[t % 2], 16 * (t // 2 + 1))
                if t >= 2:
                    pool.wait_ge(sc_done, H * (t - 1))
                pool.tensor_scalar(pen[:, t % 2, :], row[:, t % 2, :], 0.0, OUT,
                                   ALU.is_le, ALU.mult).then_inc(pen_raw, 1)
                pool.wait_ge(pen_raw, t + 1)
                spot = pen[:, t % 2, P * t:P * t + P]
                pool.affine_select(out=spot, in_=spot, compare_op=ALU.not_equal, fill=OUT, base=0,
                                   pattern=[[-1, P]], channel_multiplier=1).then_inc(pen_done, 1)
                if t + 2 < NT:
                    pool.dma_start(row[:, t % 2, :], adj_rows[t + 2]).then_inc(row_in[t % 2], 16)

            def clean_of(b, q):
                pool.wait_ge(col_in[q], 16 * (NB + b + 1))
                if q == b:
                    spot = col[:, q, :, :]
                    pool.affine_select(out=spot, in_=spot, compare_op=ALU.not_equal, fill=0.0, base=0,
                                       pattern=[[-P, KT], [1, BLK]], channel_multiplier=-1).then_inc(clean, 1)
                else:
                    pool.sem_inc(clean, 1)

            for t in range(KT):
                pen_of(t)
            for b in range(NB):
                for q in range(NB):
                    clean_of(b, q)
                    if b + 1 < NB:
                        pen_of(KT * (b + 1) + q)

        @block.tensor
        def _(pe):
            mm, transpose = nc.tensor.matmul, nc.tensor.transpose

            pe.wait_ge(const_set, 9)
            pe.wait_ge(weights_in, 64)
            for h in range(H):
                last = transpose(ps[:, 7, h * D:(h + 1) * D], wcat[:, h * D:(h + 1) * D], ident[:, :])
            last.then_inc(wprep, 1)
            pe.wait_ge(wcopied, 1)
            for h in range(H):
                last = mm(ps[:, 6, 2 * h:2 * h + 2], stage[:, h * D:(h + 1) * D], gas[:, h, :],
                          start=True, stop=True)
            last.then_inc(wprep, 1)
            for g in range(NB):
                pe.wait_ge(p_z, g + 1)
                if g:
                    pe.wait_ge(p_ztc, g)
                for k in range(KT):
                    last = transpose(ps[:, 5, k * P:(k + 1) * P], zr[:, k, :], ident[:, :])
                last.then_inc(p_zt, 1)
                pe.wait_ge(p_ztc, g + 1)
                if g:
                    pe.wait_ge(p_msgc, g)
                for k in range(KT):
                    last = mm(ps[:, 4, k * D:(k + 1) * D], zt[:, k * P:(k + 1) * P], w0s[:, :],
                              start=True, stop=True)
                last.then_inc(p_msg, 1)

            def adj_chunk(b, j):
                q = j // KT
                if j % KT == 0:
                    pe.wait_ge(col_in[q], 16 * b + 16)
                if not (isinstance(b, int) and b == 0 and j < 4):
                    pe.wait_ge(wgt_done, NT * b + j - 3)
                for k in range(KT):
                    last = transpose(ps[:, j % 4, k * P:(k + 1) * P],
                                     col[:, q, k, (j % KT) * P:(j % KT + 1) * P], ident[:, :])
                last.then_inc(adj_t, 1)

            def sum_chunk(b, j):
                pe.wait_ge(wgt_done, NT * b + j + 1)
                mm(ps[:, 4, :], msg[:, j, :], wgt[:, j % 4, :], start=(j == 0), stop=(j == NT - 1))\
                    .then_inc(summed, 1)

            def hw_chunk(f, k):
                mm(ps[:, (7, 5, 7, 6)[k], 0:HWC], zt[:, k * P:(k + 1) * P], wcat[:, :],
                   start=True, stop=True).then_inc(f_hw, 1)

            def finish(f, step):
                if step == 3:
                    pe.wait_ge(f_xs, f + 1)
                    for k in range(KT):
                        last = transpose(ps[:, 5, k * P:(k + 1) * P], xs[:, k * P:(k + 1) * P], ident[:, :])
                    last.then_inc(f_xt, 1)
                if step == 8:
                    pe.wait_ge(f_z, f + 1)
                    for k in range(KT):
                        last = transpose(ps[:, 6, k * P:(k + 1) * P], zr[:, k, :], ident[:, :])
                    last.then_inc(f_zt, 1)
                if step == 9:
                    pe.wait_ge(f_ztc, f + 1)
                    hw_chunk(f, 0)
                    hw_chunk(f, 1)
                if step == 11:
                    pe.wait_ge(f_hwa, 2 * f + 1)
                    hw_chunk(f, 2)
                    hw_chunk(f, 3)

            def layer0(b, first):
                for j in range(NT):
                    adj_chunk(b, j)
                    if not first:
                        finish(b - 1, j)
                    if j >= 3:
                        sum_chunk(b, j - 3)
                    elif not first:
                        sum_chunk(b - 1, NT - 3 + j)

            pe.wait_ge(p_msgc, NB)
            layer0(0, True)
            with nc.tensor.Fori(1, NB) as b:
                layer0(b, False)
            for j in range(3):
                sum_chunk(NB - 1, NT - 3 + j)
            pe.wait_ge(gru_w_in, 64)
            for c in range(4):
                for g in range(3):
                    last = transpose(ps[:, c, g * D:(g + 1) * D], graw[:, c, g, :], ident[:, :])
                last.then_inc(wprep, 1)
            for step in range(NT):
                finish(NB - 1, step)

            pe.wait_ge(hu_split, 1)
            pe.wait_ge(no_self, NT)
            pe.wait_ge(wcopied, 6)
            for t in range(NT):
                for j in range(NT):
                    last = mm(ps[:, 0, t * HC:(t + 1) * HC], mask[:, j, t * P:(t + 1) * P], hu3[:, j, :],
                              start=(j == 0), stop=(j == NT - 1))
            last.then_inc(q_done, 1)
            for n in range(H * NB):
                pe.wait_ge(e_diag, n + 1)
                if n >= 4:
                    pe.wait_ge(*((e_rowa, (n - 4) // 2 + 1) if n % 2 == 0 else (e_rowv, (n - 4) // 2 + 1)))
                mm(ps[:, 1 + n % 4, :], ones[:, :], tt[:, n % 4, :], start=True, stop=True).then_inc(e_row, 1)
            pe.wait_ge(ok_min, 1)
            transpose(ps[0:1, 0, 256:256 + P], okm[:, 0:1], ident[:, :]).then_inc(ok_t, 1)
            def att_chunk(b, j):
                q = j // KT
                if j % KT == 0:
                    pe.wait_ge(clean, NB * b + q + 1)
                if not (isinstance(b, int) and b == 0 and j < 2):
                    pe.wait_ge(att_done, NT * b + j - 1)
                for k in range(KT):
                    last = transpose(ps[:, j % 2, k * P:(k + 1) * P],
                                     col[:, q, k, (j % KT) * P:(j % KT + 1) * P], ident[:, :])
                last.then_inc(att_t, 1)

            def supports(b, j, first):
                if j == 0 and not first:
                    pe.wait_ge(sup_out, 2 * b)
                pe.wait_ge(att_done, NT * b + j + 1)
                mm(ps[:, 2, :], h2[:, j, :], att[:, j % 2, :], start=(j == 0), stop=(j == NT - 1))\
                    .then_inc(ns_mm, 1)
                for h in range(H):
                    n = H * j + h
                    pe.wait_ge(u_done, H * NT * b + n + 1)
                    mm(ps[:, 3, :], hw[:, j, h * D:(h + 1) * D], uu[:, n % 4, :],
                       start=(n == 0), stop=(n == H * NT - 1)).then_inc(es_mm, 1)

            def broadcast(s):
                for k in range(KT):
                    pe.wait_ge(dg_done, KT * s + k + 1)
                    mm(ps[:, 4 + k, 0:H * P], ones[:, :], dg[:, k % 2, :, :].rearrange("p h c -> p (h c)"),
                       start=True, stop=True).then_inc(bc_done, 1)

            def gates(f, cell, part_):
                hs = h2t[:, bass.ts(f, BLK)]
                sup = gru[:, NSB + cell, :]
                ih, hh = 2 * cell, 2 * cell + 1
                if part_ == 0:
                    pe.wait_ge(sup_out, 2 * f + 2)
                    if cell == 1:
                        pe.wait_ge(g_dve, 4 * f + 2)
                        pe.wait_ge(g_act, 6 * f + 2)
                    for g in range(2):
                        mm(ps[:, 5 + g, :], wt[:, ih, g * D:(g + 1) * D], sup, start=True, stop=False)
                        mm(ps[:, 5 + g, :], wt[:, hh, g * D:(g + 1) * D], hs, start=False, stop=True)\
                            .then_inc(g_mm, 1)
                    mm(ps[:, 7, :], wt[:, hh, 2 * D:3 * D], hs, start=True, stop=True).then_inc(g_mm, 1)
                else:
                    mm(ps[:, 4, :], wt[:, ih, 2 * D:3 * D], sup, start=True, stop=True).then_inc(g_mm, 1)

            def out_transpose(f):
                pe.wait_ge(o_sum, f + 1)
                for k in range(KT):
                    last = transpose(ps[:, 5, k * P:(k + 1) * P], gru[:, ST, k * P:(k + 1) * P], ident[:, :])
                last.then_inc(o_t, 1)

            def gru_step(f, j):
                if j == 1:
                    gates(f, 0, 0)
                    gates(f, 0, 1)
                if j == 5:
                    gates(f, 1, 0)
                    gates(f, 1, 1)
                if j == 10:
                    out_transpose(f)

            def layer1(b, first, last_):
                for j in range(NT):
                    if j + 1 < NT:
                        att_chunk(b, j + 1)
                    elif not last_:
                        att_chunk(b + 1, 0)
                    supports(b, j, first)
                    if not first:
                        gru_step(b - 1, j)
                if not last_:
                    broadcast(b + 1)

            pe.wait_ge(e_rowv, H * NB // 2)
            pe.wait_ge(flag_set, 1)
            att_chunk(0, 0)
            broadcast(0)
            layer1(0, True, False)
            with nc.tensor.Fori(1, NB - 1) as b:
                layer1(b, False, False)
            layer1(NB - 1, False, True)
            for j in range(NT):
                gru_step(NB - 1, j)

        @block.scalar
        def _(act):
            activation = nc.scalar.activation

            act.wait_ge(const_set, 9)
            act.wait_ge(p_stat, 1)
            activation(rstd[:, :], mv[:, :, 1], ACT.Ln, bias=epsb[:, :]).then_inc(recip_ln0, 1)
            act.wait_ge(recip_ln0, 1)
            activation(rstd[:, :], rstd[:, :], ACT.Exp, scale=-0.5).then_inc(p_rstd, 1)
            act.wait_ge(wprep, 1)
            activation(stage, ps[:, 7, 0:H * D], ACT.Copy).then_inc(wcopied, 1)
            act.wait_ge(wprep, 2)
            activation(wcat[:, H * D:HWC], ps[:, 6, 0:2 * H], ACT.Copy).then_inc(wcopied, 1)
            for g in range(NB):
                act.wait_ge(p_zt, g + 1)
                if g:
                    act.wait_ge(p_msg, g)
                activation(zt, ps[:, 5, :], ACT.Copy).then_inc(p_ztc, 1)

            def reciprocal(b, j):
                u = NT * b + j
                act.wait_ge(adj_t, u + 1)
                if not (isinstance(b, int) and b == 0 and j < 4):
                    act.wait_ge(sq_done, u - 3)
                activation(rec[:, j % 4, :], ps[:, j % 4, :], ACT.Ln, bias=tinyb[:, :]).then_inc(ln_adj, 1)
                act.wait_ge(ln_adj, u + 1)
                activation(rec[:, j % 4, :], rec[:, j % 4, :], ACT.Exp, scale=-1.0).then_inc(recip, 1)

            def sensitivity(b, j):
                act.wait_ge(sq_done, NT * b + j + 1)
                activation(wgt[:, j % 4, :], wgt[:, j % 4, :], ACT.Exp, bias=two[:, :], scale=-2.0)\
                    .then_inc(sens, 1)

            def finish(f, step):
                if step == 3:
                    act.wait_ge(summed, NT * f + NT)
                    activation(xs, ps[:, 4, :], ACT.Copy).then_inc(f_xs, 1)
                if step == 5:
                    act.wait_ge(f_stat, f + 1)
                    activation(rstd[:, 0:KT], mv[:, 0:KT, 1], ACT.Ln, bias=epsb[:, :]).then_inc(f_ln, 1)
                    act.wait_ge(f_ln, f + 1)
                    activation(rstd[:, 0:KT], rstd[:, 0:KT], ACT.Exp, scale=-0.5).then_inc(f_rstd, 1)
                if step == 8:
                    act.wait_ge(f_zt, f + 1)
                    act.wait_ge(f_keep, 2 * f + 2)
                    activation(zt, ps[:, 6, :], ACT.Copy).then_inc(f_ztc, 1)
                if step in (10, 12):
                    k = step - 10
                    act.wait_ge(f_hw, KT * f + k + 1)
                    activation(hw[:, bass.ds(KT * f + k, 1), :], ps[:, 7:8, 0:HWC], ACT.Copy).then_inc(f_hwa, 1)

            def layer0(b, first):
                for j in range(NT):
                    if not first:
                        finish(b - 1, j)
                    reciprocal(b, j)
                    if j:
                        sensitivity(b, j - 1)
                    elif not first:
                        sensitivity(b - 1, NT - 1)

            layer0(0, True)
            with nc.scalar.Fori(1, NB) as b:
                layer0(b, False)
            sensitivity(NB - 1, NT - 1)
            for step in range(NT):
                finish(NB - 1, step)
                if step == 3:
                    for c in range(4):
                        act.wait_ge(wprep, 3 + c)
                        activation(wt[:, c, :], ps[:, c, 0:NG], ACT.Copy).then_inc(wcopied, 1)

            for n in range(0, H * NB, 2):
                act.wait_ge(e_row, n + 1)
                activation(neb[:, n // NB, (n % NB) * BLK:(n % NB + 1) * BLK], ps[:, 1 + n % 4, :],
                           ACT.Copy).then_inc(e_rowa, 1)

            def denominator(s, n):
                act.wait_ge(max_done, KT * H * s + n + 1)
                view = sc[:, n % 2, :]
                activation(view, view, ACT.Sigmoid, bias=negmc[:, n:n + 1], scale=-1.0,
                           accum_out=den[:, n:n + 1]).then_inc(den_done, 1)

            def logarithms(s):
                act.wait_ge(den_done, KT * H * s + KT * H)
                activation(den[:, :], den[:, :], ACT.Ln, scale=H * math.exp(2 * C)).then_inc(ln_done, 1)

            def copy_nml(s):
                for k in range(KT):
                    act.wait_ge(bc_done, KT * s + k + 1)
                    activation(nmb[:, :, k * P:(k + 1) * P],
                               ps[:, 4 + k, 0:H * P].rearrange("p (h c) -> p h c", h=H),
                               ACT.Copy).then_inc(nmb_done, 1)

            def copy_att(b, j):
                u = NT * b + j
                act.wait_ge(att_t, u + 1)
                if not (isinstance(b, int) and b == 0 and j < 2):
                    act.wait_ge(u_done, H * u - H)
                    act.wait_ge(ns_mm, u - 1)
                activation(att[:, j % 2, :], ps[:, j % 2, :], ACT.Copy).then_inc(att_done, 1)

            def attention(b, j):
                for h in range(H):
                    n = H * j + h
                    if n == 0:
                        act.wait_ge(nmb_done, KT * b + KT)
                    if not (isinstance(b, int) and b == 0 and n < 4):
                        act.wait_ge(u_done, H * NT * b + n - 3)
                    activation(tt[:, n % 4, :], nmb[:, h, :], ACT.Sigmoid, bias=ew[:, h, j:j + 1])\
                        .then_inc(t_done, 1)

            def gru_step(f, j):
                if j == 1:
                    act.wait_ge(ns_mm, NT * f + NT)
                    activation(gru[:, NSB, :], ps[:, 2, :], ACT.Copy).then_inc(sup_out, 1)
                    act.wait_ge(es_mm, H * NT * f + H * NT)
                    activation(gru[:, ESB, :], ps[:, 3, :], ACT.Copy, scale=math.exp(C)).then_inc(sup_out, 1)
                if j in (2, 6):
                    c = j // 5
                    act.wait_ge(g_mm, 8 * f + 4 * c + 2)
                    if c:
                        act.wait_ge(vg, OWN * f + CELL)
                    activation(gru[:, TR, :], ps[:, 5, :], ACT.Sigmoid, bias=gb[:, c, 0:1])\
                        .then_inc(g_act, 1)
                    activation(gru[:, TZ, :], ps[:, 6, :], ACT.Sigmoid, bias=gb[:, c, 1:2])\
                        .then_inc(g_act, 1)
                if j in (5, 9):
                    c = j // 9
                    act.wait_ge(g_dve, 4 * f + 2 * c + 2)
                    activation(gru[:, NN, :], gru[:, UV, :], ACT.Tanh, bias=bi[:, 2 * c, 2:3])\
                        .then_inc(g_act, 1)

            def layer1(b, first, last_):
                for j in range(NT):
                    if not first:
                        gru_step(b - 1, j)
                    copy_att(b, j)
                    attention(b, j)
                    if not last_ and 0 < j <= KT * H:
                        denominator(b + 1, j - 1)
                if not last_:
                    logarithms(b + 1)
                    copy_nml(b + 1)

            for n in range(KT * H):
                denominator(0, n)
            logarithms(0)
            copy_nml(0)
            layer1(0, True, False)
            with nc.scalar.Fori(1, NB - 1) as b:
                layer1(b, False, False)
            layer1(NB - 1, False, True)
            for j in range(NT):
                gru_step(NB - 1, j)

        @block.vector
        def _(dve):
            v = nc.vector

            held = [0]

            def hold(b):
                if not isinstance(b, int):
                    held[0] = (held[0] + 1) % 16
                    v.memset(unused[:, held[0]:held[0] + 1], 0.0)

            def chain(semaphore, count):
                made = [count]

                def step(ins):
                    made[0] = made[0] + 1
                    ins.then_inc(semaphore, 1)
                    dve.wait_ge(semaphore, made[0])
                return step

            def refine(step, r, m):
                w_ = nwt[:, 0:r.shape[1]]
                step(v.scalar_tensor_tensor(w_, m, EPS, r, ALU.add, ALU.mult))
                step(v.tensor_tensor(w_, w_, r, ALU.mult))
                step(v.tensor_scalar(w_, w_, -0.5, 1.5, ALU.mult, ALU.add))
                step(v.tensor_tensor(r, r, w_, ALU.mult))

            def add_bias(g):
                dve.wait_ge(p_msg, g + 1)
                v.tensor_tensor(msg[:, KT * g:KT * g + KT, :],
                                ps[:, 4, :].rearrange("p (k d) -> p k d", k=KT),
                                b0s[:, :].rearrange("p (o d) -> p o d", o=1).broadcast_to([P, KT, D]),
                                ALU.add).then_inc(p_msgc, 1)

            dve.wait_ge(x_in, 16)
            for t in range(NT):
                last = v.bn_stats(stat[:, t, :], xb[:, t, :])
            pro = chain(vp, 0)
            pro(last)
            for t in range(NT):
                last = v.bn_aggr(mv[:, t, :], stat[:, t, :])
            last.then_inc(p_stat, 1)
            dve.wait_ge(p_rstd, 1)
            refine(pro, rstd[:, :], mv[:, :, 1])
            for g in range(NB):
                if g:
                    dve.wait_ge(p_zt, g)
                for k in range(KT):
                    t = KT * g + k
                    last = v.tensor_scalar(zr[:, k, :], xb[:, t, :], mv[:, t, 0:1], rstd[:, t:t + 1],
                                           ALU.subtract, ALU.mult)
                pro(last)
                v.tensor_scalar(zr, zr, 0.0, None, ALU.max).then_inc(p_z, 1)
                if g:
                    add_bias(g - 1)
            add_bias(NB - 1)
            dve.wait_ge(diag_in, 80)
            for c in range(2):
                pro(v.tensor_tensor(gb[:, c, :], bi[:, 2 * c, 0:2], bi[:, 2 * c + 1, 0:2], ALU.add))

            def squared(b, j):
                u = NT * b + j
                dve.wait_ge(recip, u + 1)
                if not (isinstance(b, int) and b == 0 and j < 4):
                    dve.wait_ge(mask_kept, u - 3)
                hold(b)
                v.tensor_scalar(mstage[:, j % 4, :], ps[:, j % 4, :], HUGE, 1.0, ALU.mult, ALU.min,
                                saturate=False).then_inc(mask_done, 1)
                if not (isinstance(b, int) and b == 0 and j < 4):
                    dve.wait_ge(summed, u - 3)
                r = rec[:, j % 4, :]
                v.scalar_tensor_tensor(wgt[:, j % 4, :], r, -2.0, r, ALU.add, ALU.mult).then_inc(sq_done, 1)

            def weigh(b, j):
                dve.wait_ge(sens, NT * b + j + 1)
                w_ = wgt[:, j % 4, :]
                v.scalar_tensor_tensor(w_, ps[:, j % 4, :], 1.0, w_, ALU.is_lt, ALU.mult).then_inc(wgt_done, 1)

            FIN = 8

            def finish(f, step):
                if step == 4:
                    dve.wait_ge(f_xt, f + 1)
                    fin = chain(vf, FIN * f)
                    dve.wait_ge(f_keep, 2 * f + 1)
                    rows = xb[:, bass.ts(f, KT), :]
                    fin(v.tensor_tensor(zr, ps[:, 5, :].rearrange("p (k d) -> p k d", k=KT), rows, ALU.add))
                    hold(f)
                    fin(v.tensor_copy(rows, zr))
                    for k in range(KT):
                        last = v.bn_stats(stat[:, k, :], zr[:, k, :])
                    fin(last)
                    hold(f)
                    for k in range(KT):
                        last = v.bn_aggr(mv[:, k, :], stat[:, k, :])
                    last.then_inc(f_stat, 1)
                if step == 6:
                    dve.wait_ge(f_rstd, f + 1)
                    fin = chain(vf, FIN * f + 3)
                    refine(fin, rstd[:, 0:KT], mv[:, 0:KT, 1])
                    for k in range(KT):
                        last = v.tensor_scalar(zr[:, k, :], zr[:, k, :], mv[:, k, 0:1],
                                               rstd[:, k:k + 1], ALU.subtract, ALU.mult)
                    fin(last)
                    v.tensor_scalar(zr, zr, 0.0, None, ALU.max).then_inc(f_z, 1)
                if step in (10, 12):
                    k = step - 9
                    dve.wait_ge(f_hw, KT * f + k + 1)
                    v.tensor_copy(hw[:, bass.ds(KT * f + k, 1), :], ps[:, (7, 5, 7, 6)[k]:(7, 5, 7, 6)[k] + 1, 0:HWC])\
                        .then_inc(f_hwv, 1)

            def layer0(b, first):
                for j in range(NT):
                    if j >= 1:
                        squared(b, j - 1)
                    elif not first:
                        squared(b - 1, NT - 1)
                    if j >= 2:
                        weigh(b, j - 2)
                    elif not first:
                        weigh(b - 1, NT - 2 + j)
                    if not first:
                        finish(b - 1, j)

            layer0(0, True)
            with nc.vector.Fori(1, NB) as b:
                layer0(b, False)
            squared(NB - 1, NT - 1)
            weigh(NB - 1, NT - 2)
            weigh(NB - 1, NT - 1)
            for step in range(NT):
                finish(NB - 1, step)

            tr = chain(vt, 0)
            dve.wait_ge(f_hwa, NT // 2)
            dve.wait_ge(f_hwv, NT // 2)
            hu = hw[:, :, H * D:H * D + 2 * H].rearrange("p t (h s) -> p t h s", s=2)[:, :, :, 0]
            tr(v.tensor_copy(hu3[:, :, 0:H], hu))
            tr(v.tensor_tensor(hur[:, 0], hu, hu3[:, :, 0:H], ALU.subtract))
            tr(v.tensor_copy(hu3[:, :, H:2 * H], hur[:, 0]))
            tr(v.tensor_tensor(hur[:, 1], hur[:, 0], hu3[:, :, H:2 * H], ALU.subtract))
            v.tensor_copy(hu3[:, :, 2 * H:3 * H], hur[:, 1]).then_inc(hu_split, 1)

            dve.wait_ge(q_done, 1)
            sums = ps[:, 0, 0:NT * HC].rearrange("p (t c) -> p t c", t=NT)
            tr(v.tensor_reduce(qs[:, :, :], sums[:, :, 0:3 * H].rearrange("p t (s h) -> p t h s", s=3),
                               AX.X, ALU.add))
            v.scalar_tensor_tensor(ew[:, :, :], qs[:, :, :].rearrange("p t h -> p h t"), 0.2,
                                   qs[:, :, :].rearrange("p t h -> p h t"), ALU.mult, ALU.max).then_inc(e_done, 1)
            dve.wait_ge(e_done, 1)

            def copy_row(n):
                dve.wait_ge(e_row, n + 1)
                v.tensor_copy(neb[:, n // NB, (n % NB) * BLK:(n % NB + 1) * BLK], ps[:, 1 + n % 4, :])\
                    .then_inc(e_rowv, 1)

            def spread(m):
                return m.rearrange("p (o c) -> p o c", o=1)

            for n in range(H * NB):
                if n >= 4:
                    dve.wait_ge(e_row, n - 3)
                k = n % NB
                v.tensor_tensor(tt[:, n % 4, :].rearrange("p (k c) -> p k c", k=KT),
                                spread(nident[:, :]).broadcast_to([P, KT, P]),
                                ew[:, n // NB, KT * k:KT * k + KT].rearrange("p (k o) -> p k o", o=1)
                                .broadcast_to([P, KT, P]), ALU.mult).then_inc(e_diag, 1)
                if n >= 2 and n % 2 == 0:
                    copy_row(n - 1)
            copy_row(H * NB - 1)

            v.tensor_scalar(okc[:, 0, :], sums[:, :, 3 * H], 0.0, None, ALU.is_ge)
            tr(v.tensor_scalar(okc[:, 1, :], de[:, :], 0.0, None, ALU.is_ge))
            v.tensor_reduce(okm[:, 0:1], okc[:, :, :], AX.XY, ALU.min).then_inc(ok_min, 1)
            dve.wait_ge(ok_t, 1)
            tr(v.tensor_reduce(okm[0:1, 1:2], ps[0:1, 0, 256:256 + P], AX.X, ALU.min))
            v.tensor_scalar(flag[:, :], okm[0:1, 1:2], 0.5, None, ALU.is_lt).then_inc(flag_set, 1)

            def scores(s, n):
                t, h = KT * s + n // H, n % H
                if n % H == 0:
                    dve.wait_ge(pen_done, t + 1)
                if not (isinstance(s, int) and s == 0 and n < 2):
                    dve.wait_ge(den_done, KT * H * s + n - 1)
                hold(s)
                v.tensor_tensor_reduce(out=sc[:, n % 2, :], in0=pen[:, (n // H) % 2, :], in1=neb[:, h, :],
                                       scale=1.0, scalar=3.0e38, op0=ALU.add, op1=ALU.min,
                                       accum_out=negm[:, n:n + 1]).then_inc(sc_done, 1)

            def maximum(s, n):
                dve.wait_ge(sc_done, KT * H * s + n + 1)
                v.tensor_scalar(negmc[:, n:n + 1], negm[:, n:n + 1], -C, None, ALU.add).then_inc(max_done, 1)

            def diagonals(s):
                dve.wait_ge(ln_done, s + 1)
                v.tensor_tensor(nml[:, :], negm[:, :], den[:, :], ALU.subtract).then_inc(nml_done, 1)
                dve.wait_ge(nml_done, s + 1)
                for k in range(KT):
                    if not (isinstance(s, int) and s == 0 and k < 2):
                        dve.wait_ge(bc_done, KT * s + k - 1)
                    v.tensor_tensor(dg[:, k % 2, :, :], spread(ident[:, :]).broadcast_to([P, H, P]),
                                    nml[:, H * k:H * k + H].rearrange("p (h o) -> p h o", o=1)
                                    .broadcast_to([P, H, P]), ALU.mult).then_inc(dg_done, 1)

            def attend(b, j):
                dve.wait_ge(att_done, NT * b + j + 1)
                for h in range(H):
                    n = H * j + h
                    dve.wait_ge(t_done, H * NT * b + n + 1)
                    if not (isinstance(b, int) and b == 0 and n < 4):
                        dve.wait_ge(es_mm, H * NT * b + n - 3)
                    v.tensor_tensor(uu[:, n % 4, :], tt[:, n % 4, :], att[:, j % 2, :],
                                    ALU.mult).then_inc(u_done, 1)

            def gru_step(f, j):
                if j in (3, 7):
                    c = j // 7
                    dve.wait_ge(g_act, 6 * f + 3 * c + 1)
                    dve.wait_ge(g_mm, 8 * f + 4 * c + 3)
                    v.scalar_tensor_tensor(gru[:, UV, :], ps[:, 7, :], bi[:, 2 * c + 1, 2:3], gru[:, TR, :],
                                           ALU.add, ALU.mult).then_inc(g_dve, 1)
                if j in (4, 8):
                    c = j // 8
                    dve.wait_ge(g_mm, 8 * f + 4 * c + 4)
                    dve.wait_ge(g_dve, 4 * f + 2 * c + 1)
                    v.tensor_tensor(gru[:, UV, :], gru[:, UV, :], ps[:, 4, :], ALU.add).then_inc(g_dve, 1)
                if j in (5, 9):
                    c = j // 9
                    own = chain(vg, OWN * f + CELL * c)
                    dve.wait_ge(g_act, 6 * f + 3 * c + 3)
                    own(v.tensor_tensor(gru[:, DD, :], h2t[:, bass.ts(f, BLK)], gru[:, NN, :], ALU.subtract))
                    own(v.tensor_tensor(gru[:, DD, :], gru[:, TZ, :], gru[:, DD, :], ALU.mult))
                    own(v.tensor_tensor(gru[:, OE if c == 0 else ST, :], gru[:, DD, :], gru[:, NN, :], ALU.add))
                if j == 10:
                    dve.wait_ge(vg, OWN * f + OWN)
                    v.tensor_tensor(gru[:, ST, :], gru[:, ST, :], gru[:, OE, :], ALU.add).then_inc(o_sum, 1)
                if j == 11:
                    dve.wait_ge(o_t, f + 1)
                    dve.wait_ge(stored, 16 * f + 16)
                    for k in range(KT):
                        last = v.scalar_tensor_tensor(osb[:, k:k + 1, :], ps[:, 5:6, k * D:(k + 1) * D],
                                                      de[:, bass.ds(KT * f + k, 1)],
                                                      xb[:, bass.ds(KT * f + k, 1), :], ALU.mult, ALU.add)
                    last.then_inc(o_done, 1)

            def layer1(b, first, last_):
                for j in range(NT):
                    if not last_ and j < KT * H:
                        scores(b + 1, j)
                    attend(b, j)
                    if not last_ and j < KT * H:
                        maximum(b + 1, j)
                    if not first:
                        gru_step(b - 1, j)
                if not last_:
                    diagonals(b + 1)

            for n in range(KT * H):
                scores(0, n)
                if n:
                    maximum(0, n - 1)
            maximum(0, KT * H - 1)
            diagonals(0)
            layer1(0, True, False)
            with nc.vector.Fori(1, NB - 1) as b:
                layer1(b, False, False)
            layer1(NB - 1, False, True)
            for j in range(NT):
                gru_step(NB - 1, j)


_INS = ["x", "adj", "L0_gnn_W", "L0_gnn_B", "L1_gnn_gat_W", "L1_gnn_gat_a",
        "L1_gnn_edge_Wih", "L1_gnn_edge_Whh", "L1_gnn_edge_bih", "L1_gnn_edge_bhh",
        "L1_gnn_node_Wih", "L1_gnn_node_Whh", "L1_gnn_node_bih", "L1_gnn_node_bhh"]


def kernel(**inputs):
    import concourse.bacc as _bacc
    from concourse.bass_utils import run_bass_kernel_spmd as _run

    nc = _bacc.Bacc("TRN2", target_bir_lowering=False, num_devices=1)
    arrays, args = {}, []
    for name in _INS:
        a = np.ascontiguousarray(inputs[name])
        arrays[f"in_{name}"] = a
        args.append(nc.dram_tensor(f"in_{name}", a.shape, mybir.dt.from_np(a.dtype), kind="ExternalInput").ap())
    args.append(nc.dram_tensor("out_x", (N, D), F32, kind="ExternalOutput").ap())
    program(nc, *args)
    r = _run(nc, [arrays], core_ids=[0])
    return r.results[0]["out_x"]
```

```python
import math
from contextlib import ExitStack

import numpy as np
import concourse.bass as bass
from concourse import mybir

F32 = mybir.dt.float32
BF16 = mybir.dt.bfloat16
F8 = mybir.dt.float8e5
I32 = mybir.dt.int32
ALU = mybir.AluOpType
ACT = mybir.ActivationFunctionType
AX = mybir.AxisListType

N, D, H, P = 2048, 128, 3, 128
NT = N // P
BLK = 512
NB = N // BLK
KT = BLK // P
NG = 3 * D
HWC = H * D + 2 * H
HC = 3 * H + 1
EPS = 1e-5
TINY = 2.0 ** -60
HUGE = 2.0 ** 127
C = 17.375
OUT = 2.0 ** 100


def program(nc, x, adj, w0, b0, gat_w, gat_a, e_wih, e_whh, e_bih, e_bhh,
            n_wih, n_whh, n_bih, n_bhh, out):
    ctx = ExitStack()
    with ctx:
        def sb(name, shape, dt=F32):
            return ctx.enter_context(nc.sbuf_tensor(name, shape, dt))

        def sem(name):
            return ctx.enter_context(nc.semaphore(name))

        xb = sb("xb", [P, NT, D])
        h2 = sb("h2", [P, NT, D])
        h2t = sb("h2t", [P, N])
        hw = sb("hw", [P, NT, HWC])
        col = sb("col", [P, NB, KT, BLK])
        row = sb("row", [P, 2, N])
        pen = sb("pen", [P, 2, N], BF16)
        sc = sb("sc", [P, 2, N])
        ident = sb("ident", [P, P])
        nident = sb("nident", [P, P])
        ones = sb("ones", [P, P])
        offdiag = sb("offdiag", [P, P], BF16)
        outdiag = sb("outdiag", [P, P], BF16)
        wcat = sb("wcat", [P, HWC])
        w0s = sb("w0s", [P, D])
        b0s = sb("b0s", [P, D])
        gas = sb("gas", [P, H, 2])
        de = sb("de", [P, NT])
        wt = sb("wt", [P, 4, NG])
        bi = sb("bi", [P, 4, 3])
        gb = sb("gb", [P, 2, 2])
        stat = sb("stat", [P, NT, 6])
        mv = sb("mv", [P, NT, 2])
        var = sb("var", [P, NT])
        rstd = sb("rstd", [P, NT])
        nwt = sb("nwt", [P, NT])
        hu3 = sb("hu3", [P, NT, HC], BF16)
        hur = sb("hur", [P, 2, NT, H])
        ew = sb("ew", [P, H, NT])
        nege = sb("nege", [P, H, NT])
        qs = sb("qs", [P, NT, H])
        negm = sb("negm", [P, KT * H])
        den = sb("den", [P, KT * H])
        negmc = sb("negmc", [P, KT * H])
        nml = sb("nml", [P, KT * H])
        okc = sb("okc", [P, 2, NT])
        okm = sb("okm", [P, 4])
        flag = sb("flag", [1, 1], I32)
        unused = sb("unused", [1, 16])
        epsb = sb("epsb", [P, 1])
        tinyb = sb("tinyb", [P, 1])
        two = sb("two", [P, 1])

        arena = sb("arena", [P, 17920])

        def part(start, *dims):
            size = int(np.prod(dims))
            view = arena[:, start:start + size]
            if len(dims) == 2:
                view = view.rearrange("p (a b) -> p a b", a=dims[0])
            if len(dims) == 3:
                view = view.rearrange("p (a b c) -> p a b c", a=dims[0], b=dims[1])
            return view

        mask = part(0, NT * N // 4).bitcast(F8).rearrange("p (a b) -> p a b", a=NT)
        rec = part(8192, 4, BLK)
        wgt = part(10240, 4, BLK)
        msg = part(12288, NT, D)
        mstage = part(15872, BLK).bitcast(F8).rearrange("p (a b) -> p a b", a=4)
        xs = part(14336, BLK)
        zr = part(14848, KT, D)
        zt = part(15360, BLK)
        stage = part(14336, 3 * P)
        graw = sc[:, 0, 0:4 * NG].rearrange("p (c g d) -> p c g d", c=4, g=3)

        neb = part(0, H, N)
        nmb = part(6144, H, BLK)
        tt = part(7680, 4, BLK)
        uu = part(9728, 4, BLK)
        att = part(11776, 2, BLK)
        gru = part(12800, 9, BLK)
        osb = part(17408, KT, D)
        NSB, ESB, TR, TZ, UV, NN, DD, OE, ST = range(9)

        ps = ctx.enter_context(nc.psum_tensor("ps", [P, 8, 512], F32))

        x_in = sem("x_in")
        weights_in = sem("weights_in")
        gru_w_in = sem("gru_w_in")
        diag_in = sem("diag_in")
        col_in = [sem(f"col_in{s}") for s in range(NB)]
        row_in = [sem(f"row_in{s}") for s in range(2)]
        stored = sem("stored")
        const_set = sem("const_set")
        wprep = sem("wprep")
        wcopied = sem("wcopied")
        p_stat = sem("p_stat")
        recip_ln0 = sem("recip_ln0")
        p_rstd = sem("p_rstd")
        p_z = sem("p_z")
        p_zt = sem("p_zt")
        p_ztc = sem("p_ztc")
        p_msg = sem("p_msg")
        p_msgc = sem("p_msgc")
        vp = sem("vp")
        adj_t = sem("adj_t")
        ln_adj = sem("ln_adj")
        recip = sem("recip")
        mask_done = sem("mask_done")
        mask_kept = sem("mask_kept")
        sq_done = sem("sq_done")
        sens = sem("sens")
        wgt_done = sem("wgt_done")
        summed = sem("summed")
        f_xs = sem("f_xs")
        f_xt = sem("f_xt")
        f_stat = sem("f_stat")
        f_ln = sem("f_ln")
        f_rstd = sem("f_rstd")
        f_z = sem("f_z")
        f_zt = sem("f_zt")
        f_ztc = sem("f_ztc")
        f_keep = sem("f_keep")
        f_hw = sem("f_hw")
        f_hwa = sem("f_hwa")
        f_hwv = sem("f_hwv")
        vf = sem("vf")
        no_self = sem("no_self")
        hu_split = sem("hu_split")
        vt = sem("vt")
        q_done = sem("q_done")
        e_done = sem("e_done")
        e_row = sem("e_row")
        e_rowa = sem("e_rowa")
        e_rowv = sem("e_rowv")
        ok_min = sem("ok_min")
        ok_t = sem("ok_t")
        flag_set = sem("flag_set")
        clean = sem("clean")
        pen_raw = sem("pen_raw")
        pen_done = sem("pen_done")
        pen_own = sem("pen_own")
        max_done = sem("max_done")
        sc_done = sem("sc_done")
        den_done = sem("den_done")
        ln_done = sem("ln_done")
        nml_done = sem("nml_done")
        bc_done = sem("bc_done")
        nmb_done = sem("nmb_done")
        att_t = sem("att_t")
        att_done = sem("att_done")
        t_done = sem("t_done")
        u_done = sem("u_done")
        ns_mm = sem("ns_mm")
        es_mm = sem("es_mm")
        sup_out = sem("sup_out")
        g_mm = sem("g_mm")
        g_act = sem("g_act")
        g_dve = sem("g_dve")
        vg = sem("vg")
        o_sum = sem("o_sum")
        o_t = sem("o_t")
        o_done = sem("o_done")

        adj_cols = adj.rearrange("(b k p) (q c) -> b q p k c", k=KT, p=P, q=NB)
        adj_rows = adj.rearrange("(t p) n -> t p n", p=P)
        out_blocks = out.rearrange("(b k p) d -> b p k d", k=KT, p=P)

        CELL = 3
        OWN = 2 * CELL

        general_step = sem("general_step")
        g_x_in = sem("g_x_in")
        g_row_in = sem("g_row_in")
        g_stored = sem("g_stored")
        a_row, w_row = row[:, 0, :], row[:, 1, :]
        pos, neg = sc[:, 0, :], sc[:, 1, :]
        none = col[:, 0, :, :].rearrange("p k c -> p (k c)")
        score = col[:, 1, :, :].rearrange("p k c -> p (k c)")
        score2 = col[:, 2, :, :].rearrange("p k c -> p (k c)")
        e_all = part(0, 2 * H, N)
        g_msg = part(12288, NT, D)
        quad = part(14336, BLK)
        cur, z = part(14848, D), part(14976, D)
        zt_g = part(15104, P)
        e_col = part(15232, 2 * H, NT)
        dg6 = part(15328, 2 * H, P)
        sup2 = part(16096, 2, P)
        sup_rows = part(16352, 2, D)
        g_r, g_z, g_n, g_d, g_sum, g_out = (part(16608 + k * P, P) for k in range(6))
        nbr = part(17376, 2 * H)
        g_small = part(17400, 8)
        G_MAX, G_BIAS, G_DEN, G_RDEN = range(4)

        def product_steps(tag):
            return [f"{tag} {what} {q}" for q in range(NB) for what in ("transpose", "copy", "multiply")]

        LN = ["stats", "aggregate", "ln", "rsqrt", "newton 0", "newton 1", "newton 2", "newton 3",
              "normalise", "relu", "transpose z", "copy z"]
        MESSAGES = ["fetch"] + LN + ["times w0", "add b0"]
        WEIGHTS = (["square", "clamp", "reciprocal", "r", "q", "exp", "below 1", "not 0"] + product_steps("sum")
                   + ["x1", "keep x1"] + LN + ["keep h2", "keep h2t", "times W", "keep hw"])
        SIGNS = ["no diagonal", "pos", "neg"]
        NEIGHBOURS = (SIGNS + product_steps("plus") + product_steps("minus")
                      + ["keep plus", "e_plus", "e_minus", "leaky plus", "leaky minus"])
        SPREAD = ["diagonals", "spread", "copy plus", "copy minus"]
        HEAD = ["plus score", "minus score", "both", "outside", "max", "bias", "exp", "denominator",
                "reciprocal", "probability"]
        CELLS = ["gates", "sigmoid r", "sigmoid z", "times r", "add in", "tanh", "h - n", "times z", "add n"]
        ATTEND = SIGNS + ["none"] + product_steps("node")
        for h in range(H):
            ATTEND += [f"{h} {name}" for name in HEAD] + product_steps(f"{h} edge")
        ATTEND += ["keep node", "keep edge", "transpose supports", "copy supports"]
        for c in range(2):
            ATTEND += [f"{c} {name}" for name in CELLS]
        ATTEND += ["add cells", "transpose out", "out"]
        S1 = 1
        S2 = S1 + len(MESSAGES) * NT
        S3 = S2 + len(WEIGHTS) * NT
        S4 = S3 + len(NEIGHBOURS) * NT
        S5 = S4 + len(SPREAD) * NT

        block = ctx.enter_context(nc.Block())

        @block.sync
        def _(sp):
            sp.sem_inc(stored, 16)
            sp.dma_start(xb[:, :, :], x.rearrange("(t p) d -> p t d", p=P)).then_inc(x_in, 16)
            for q in range(NB):
                sp.dma_start(col[:, q, :, :], adj_cols[0, q]).then_inc(col_in[q], 16)
            with nc.sync.Fori(1, NB) as b:
                for q in range(NB):
                    sp.wait_ge(adj_t, NT * b - NT + KT * q + KT)
                    sp.dma_start(col[:, q, :, :], adj_cols[bass.ds(b, 1), q, :, :, :]
                                 .rearrange("o p k c -> (o p) k c")).then_inc(col_in[q], 16)
            for q in range(NB):
                sp.wait_ge(adj_t, NT * (NB - 1) + KT * q + KT)
                sp.dma_start(col[:, q, :, :], adj_cols[0, q]).then_inc(col_in[q], 16)
            def next_block(b, first):
                for q in range(NB):
                    if q == NB - 1 and not first:
                        store(b - 1)
                    sp.wait_ge(att_t, NT * b + KT * q + KT)
                    sp.dma_start(col[:, q, :, :], adj_cols[bass.ds(b + 1, 1), q, :, :, :]
                                 .rearrange("o p k c -> (o p) k c")).then_inc(col_in[q], 16)

            def store(f):
                sp.wait_ge(o_done, f + 1)
                sp.dma_start(out_blocks[bass.ds(f, 1), :, :, :].rearrange("o p k d -> (o p) k d"),
                             osb).then_inc(stored, 16)

            next_block(0, True)
            with nc.sync.Fori(1, NB - 1) as b:
                next_block(b, False)
            store(NB - 2)
            store(NB - 1)
            sp.wait_ge(stored, 16 * NB + 16)

            sp.wait_ge(flag_set, 1)
            signed = nc.sync.value_load(flag[0:1, 0:1], min_val=0, max_val=1)
            with nc.sync.If(signed != 0):
                sp.dma_start(xb[:, :, :], x.rearrange("(t p) d -> p t d", p=P)).then_inc(g_x_in, 16)
                sp.sem_inc(general_step, 1)
                sp.sem_inc(g_stored, 16)

                def load_rows(t, free):
                    sp.wait_ge(general_step, free)
                    sp.dma_start(row[:, 0:1, :], adj_rows[bass.ds(t, 1), :, :]
                                 .rearrange("o p n -> p o n")).then_inc(g_row_in, 16)

                for start, steps in ((S2, WEIGHTS), (S3, NEIGHBOURS)):
                    with nc.sync.Fori(0, NT) as t:
                        load_rows(t, len(steps) * t + start)
                with nc.sync.Fori(0, NT) as t:
                    sp.wait_ge(g_stored, 16 * t + 16)
                    load_rows(t, len(ATTEND) * t + S5)
                    sp.wait_ge(general_step, len(ATTEND) * t + S5 + len(ATTEND))
                    sp.dma_start(out[bass.ds(P * t, P), :], g_out).then_inc(g_stored, 16)
                sp.wait_ge(g_stored, 16 * NT + 16)

        @block.gpsimd
        def _(pool):
            pool.memset(ident[:, :], 0.0).then_inc(const_set, 1)
            pool.memset(ones[:, :], 1.0).then_inc(const_set, 1)
            pool.memset(epsb[:, :], EPS).then_inc(const_set, 1)
            pool.memset(tinyb[:, :], TINY).then_inc(const_set, 1)
            pool.memset(two[:, :], -2.0).then_inc(const_set, 1)
            pool.memset(hu3[:, :, :], 1.0).then_inc(const_set, 1)
            pool.wait_ge(const_set, 6)
            pool.affine_select(out=ident[:, :], in_=ident[:, :], compare_op=ALU.not_equal, fill=1.0,
                               base=0, pattern=[[-1, P]], channel_multiplier=1).then_inc(const_set, 1)
            pool.wait_ge(const_set, 7)
            pool.tensor_scalar(nident[:, :], ident[:, :], -1.0, 0.0, ALU.mult, ALU.add).then_inc(const_set, 1)
            pool.tensor_scalar(offdiag[:, :], ident[:, :], -1.0, 1.0, ALU.mult, ALU.add).then_inc(const_set, 1)

            pool.tensor_scalar(outdiag[:, :], ident[:, :], OUT, 0.0, ALU.mult, ALU.add).then_inc(const_set, 1)

            pool.dma_start(w0s[:, :], w0).then_inc(weights_in, 16)
            pool.dma_start(b0s[:, :], b0.rearrange("(o d) -> o d", o=1).broadcast_to([P, D])).then_inc(weights_in, 16)
            pool.dma_start(wcat[:, 0:H * D].rearrange("p (h d) -> p h d", h=H),
                           gat_w.rearrange("h p d -> p h d")).then_inc(weights_in, 16)
            pool.dma_start(gas[:, :, :], gat_a.rearrange("h (s p) o -> p h (s o)", s=2),
                           allow_slow_non_contiguous=True).then_inc(weights_in, 16)
            pool.dma_start(de[:, :], bass.AP(adj.tensor, 0, [[N + 1, P], [P * (N + 1), NT], [1, 1]])
                           .rearrange("p t o -> p (t o)"), allow_slow_non_contiguous=True).then_inc(diag_in, 16)
            for c, b_ in enumerate((e_bih, e_bhh, n_bih, n_bhh)):
                pool.dma_start(bi[:, c, :], b_.rearrange("(g p) -> p g", p=P),
                               allow_slow_non_contiguous=True).then_inc(diag_in, 16)

            for c, w in enumerate((e_wih, e_whh, n_wih, n_whh)):
                pool.dma_start(graw[:, c, :, :], w.rearrange("(g p) d -> p g d", p=P)).then_inc(gru_w_in, 16)
            pool.sem_inc(f_keep, 2)
            for t in range(2):
                pool.dma_start(row[:, t, :], adj_rows[t]).then_inc(row_in[t], 16)

            def keep_h2(f):
                pool.wait_ge(f_z, f + 1)
                pool.tensor_copy(h2[:, bass.ts(f, KT), :], zr).then_inc(f_keep, 1)

            def keep_h2t(f):
                pool.wait_ge(f_ztc, f + 1)
                pool.tensor_copy(h2t[:, bass.ts(f, BLK)], zt).then_inc(f_keep, 1)

            def pen_quarter(n):
                t, cols = n // NB, slice((n % NB) * BLK, (n % NB + 1) * BLK)
                pool.wait_ge(row_in[t], 16)
                pool.tensor_scalar(pen[:, t, cols], row[:, t, cols], 0.0, OUT,
                                   ALU.is_le, ALU.mult).then_inc(pen_raw, 1)

            def pen_diagonal(t):
                spot = pen[:, t % 2, P * t:P * t + P]
                pool.affine_select(out=spot, in_=spot, compare_op=ALU.not_equal, fill=OUT, base=0,
                                   pattern=[[-1, P]], channel_multiplier=1).then_inc(pen_done, 1)

            def layer0(b, first):
                for j in range(NT):
                    pool.wait_ge(mask_done, NT * b + j + 1)
                    pool.tensor_copy(mask[:, j, bass.ts(b, BLK)].bitcast(I32), mstage[:, j % 4, :].bitcast(I32))\
                        .then_inc(mask_kept, 1)
                    if first and j % 2:
                        pen_quarter(j // 2)
                    if not first and j == 8:
                        keep_h2(b - 1)
                    if not first and j == 10:
                        keep_h2t(b - 1)

            layer0(0, True)
            pool.wait_ge(pen_raw, 2 * NB)
            for t in range(2):
                pen_diagonal(t)
                pool.dma_start(row[:, t, :], adj_rows[t + 2]).then_inc(row_in[t], 16)
            with nc.gpsimd.Fori(1, NB) as b:
                layer0(b, False)
            pool.wait_ge(mask_kept, NT * NB)
            for t in range(NT):
                spot = mask[:, t, P * t:P * t + P]
                pool.tensor_tensor(spot, spot, offdiag[:, :], ALU.mult, saturate=False).then_inc(no_self, 1)
            keep_h2(NB - 1)
            keep_h2t(NB - 1)

            def pen_of(t):
                pool.wait_ge(row_in[t % 2], 16 * (t // 2 + 1))
                pool.wait_ge(sc_done, H * (t - 1))
                pool.tensor_scalar(pen[:, t % 2, :], row[:, t % 2, :], 0.0, OUT,
                                   ALU.is_le, ALU.mult).then_inc(pen_raw, 1)
                pool.wait_ge(pen_raw, 2 * NB + t - 3)
                pen_diagonal(t)
                if t + 2 < NT:
                    pool.dma_start(row[:, t % 2, :], adj_rows[t + 2]).then_inc(row_in[t % 2], 16)

            def clean_of(b, q):
                pool.wait_ge(col_in[q], 16 * (NB + b + 1))
                if q == b:
                    spot = col[:, q, :, :]
                    pool.affine_select(out=spot, in_=spot, compare_op=ALU.not_equal, fill=0.0, base=0,
                                       pattern=[[-P, KT], [1, BLK]], channel_multiplier=-1).then_inc(clean, 1)
                else:
                    pool.sem_inc(clean, 1)

            for t in range(2):
                pool.wait_ge(pen_own, t + 1)
                pool.dma_start(row[:, t, :], adj_rows[t + 4]).then_inc(row_in[t], 16)
            for b in range(NB):
                for q in range(NB):
                    clean_of(b, q)
                    if b + 1 < NB:
                        pen_of(KT * (b + 1) + q)

        @block.tensor
        def _(pe):
            mm, transpose = nc.tensor.matmul, nc.tensor.transpose

            pe.wait_ge(const_set, 9)
            pe.wait_ge(weights_in, 64)
            for h in range(H):
                last = transpose(ps[:, 7, h * D:(h + 1) * D], wcat[:, h * D:(h + 1) * D], ident[:, :])
            last.then_inc(wprep, 1)
            pe.wait_ge(wcopied, 1)
            for h in range(H):
                last = mm(ps[:, 6, 2 * h:2 * h + 2], stage[:, h * D:(h + 1) * D], gas[:, h, :],
                          start=True, stop=True)
            last.then_inc(wprep, 1)
            for g in range(NB):
                pe.wait_ge(p_z, g + 1)
                if g:
                    pe.wait_ge(p_ztc, g)
                for k in range(KT):
                    last = transpose(ps[:, 5, k * P:(k + 1) * P], zr[:, k, :], ident[:, :])
                last.then_inc(p_zt, 1)
                pe.wait_ge(p_ztc, g + 1)
                if g:
                    pe.wait_ge(p_msgc, g)
                for k in range(KT):
                    last = mm(ps[:, 4, k * D:(k + 1) * D], zt[:, k * P:(k + 1) * P], w0s[:, :],
                              start=True, stop=True)
                last.then_inc(p_msg, 1)

            def adj_chunk(b, j):
                q = j // KT
                if j % KT == 0:
                    pe.wait_ge(col_in[q], 16 * b + 16)
                if not (isinstance(b, int) and b == 0 and j < 4):
                    pe.wait_ge(wgt_done, NT * b + j - 3)
                for k in range(KT):
                    last = transpose(ps[:, j % 4, k * P:(k + 1) * P],
                                     col[:, q, k, (j % KT) * P:(j % KT + 1) * P], ident[:, :])
                last.then_inc(adj_t, 1)

            def sum_chunk(b, j):
                pe.wait_ge(wgt_done, NT * b + j + 1)
                mm(ps[:, 4, :], msg[:, j, :], wgt[:, j % 4, :], start=(j == 0), stop=(j == NT - 1))\
                    .then_inc(summed, 1)

            def hw_chunk(f, k):
                mm(ps[:, (7, 5, 7, 6)[k], 0:HWC], zt[:, k * P:(k + 1) * P], wcat[:, :],
                   start=True, stop=True).then_inc(f_hw, 1)

            def finish(f, step):
                if step == 3:
                    pe.wait_ge(f_xs, f + 1)
                    for k in range(KT):
                        last = transpose(ps[:, 5, k * P:(k + 1) * P], xs[:, k * P:(k + 1) * P], ident[:, :])
                    last.then_inc(f_xt, 1)
                if step == 8:
                    pe.wait_ge(f_z, f + 1)
                    for k in range(KT):
                        last = transpose(ps[:, 6, k * P:(k + 1) * P], zr[:, k, :], ident[:, :])
                    last.then_inc(f_zt, 1)
                if step == 9:
                    pe.wait_ge(f_ztc, f + 1)
                    hw_chunk(f, 0)
                    hw_chunk(f, 1)
                if step == 11:
                    pe.wait_ge(f_hwa, 2 * f + 1)
                    hw_chunk(f, 2)
                    hw_chunk(f, 3)

            def layer0(b, first):
                for j in range(NT):
                    adj_chunk(b, j)
                    if not first:
                        finish(b - 1, j)
                    if j >= 3:
                        sum_chunk(b, j - 3)
                    elif not first:
                        sum_chunk(b - 1, NT - 3 + j)

            pe.wait_ge(p_msgc, NB)
            layer0(0, True)
            with nc.tensor.Fori(1, NB) as b:
                layer0(b, False)
            for j in range(3):
                sum_chunk(NB - 1, NT - 3 + j)
            pe.wait_ge(gru_w_in, 64)
            for c in range(4):
                for g in range(3):
                    last = transpose(ps[:, c, g * D:(g + 1) * D], graw[:, c, g, :], ident[:, :])
                last.then_inc(wprep, 1)
            for step in range(NT):
                finish(NB - 1, step)

            pe.wait_ge(hu_split, 1)
            pe.wait_ge(no_self, NT)
            pe.wait_ge(wcopied, 6)
            for t in range(NT):
                for j in range(NT):
                    last = mm(ps[:, 0, t * HC:(t + 1) * HC], mask[:, j, t * P:(t + 1) * P], hu3[:, j, :],
                              start=(j == 0), stop=(j == NT - 1))
            last.then_inc(q_done, 1)
            pe.wait_ge(e_done, 2)
            for n in range(H * NB):
                if n >= 4:
                    pe.wait_ge(*((e_rowa, (n - 4) // 2 + 1) if n % 2 == 0 else (e_rowv, (n - 4) // 2 + 1)))
                for k in range(KT):
                    t = KT * (n % NB) + k
                    last = transpose(ps[:, 1 + n % 4, k * P:(k + 1) * P],
                                     nege[:, n // NB, t:t + 1].broadcast_to([P, P]), ident[:, :])
                last.then_inc(e_row, 1)
                if n == 5:
                    pe.wait_ge(ok_min, 1)
                    transpose(ps[0:1, 0, 256:256 + P], okm[:, 0:1], ident[:, :]).then_inc(ok_t, 1)
            def att_chunk(b, j):
                q = j // KT
                if j % KT == 0:
                    pe.wait_ge(clean, NB * b + q + 1)
                if not (isinstance(b, int) and b == 0 and j < 2):
                    pe.wait_ge(att_done, NT * b + j - 1)
                for k in range(KT):
                    last = transpose(ps[:, j % 2, k * P:(k + 1) * P],
                                     col[:, q, k, (j % KT) * P:(j % KT + 1) * P], ident[:, :])
                last.then_inc(att_t, 1)

            def supports(b, j, first):
                if j == 0 and not first:
                    pe.wait_ge(sup_out, 2 * b)
                pe.wait_ge(att_done, NT * b + j + 1)
                mm(ps[:, 2, :], h2[:, j, :], att[:, j % 2, :], start=(j == 0), stop=(j == NT - 1))\
                    .then_inc(ns_mm, 1)
                for h in range(H):
                    n = H * j + h
                    pe.wait_ge(u_done, H * NT * b + n + 1)
                    mm(ps[:, 3, :], hw[:, j, h * D:(h + 1) * D], uu[:, n % 4, :],
                       start=(n == 0), stop=(n == H * NT - 1)).then_inc(es_mm, 1)

            def broadcast(s):
                pe.wait_ge(nml_done, s + 1)
                for h in range(H):
                    for k in range(KT):
                        n = H * k + h
                        last = transpose(ps[:, 4 + h, k * P:(k + 1) * P],
                                         nml[:, n:n + 1].broadcast_to([P, P]), ident[:, :])
                    last.then_inc(bc_done, 1)

            def gates(f, cell, part_):
                hs = h2t[:, bass.ts(f, BLK)]
                sup = gru[:, NSB + cell, :]
                ih, hh = 2 * cell, 2 * cell + 1
                if part_ == 0:
                    pe.wait_ge(sup_out, 2 * f + 2)
                    if cell == 1:
                        pe.wait_ge(g_dve, 4 * f + 2)
                        pe.wait_ge(g_act, 6 * f + 2)
                    for g in range(2):
                        mm(ps[:, 5 + g, :], wt[:, ih, g * D:(g + 1) * D], sup, start=True, stop=False)
                        mm(ps[:, 5 + g, :], wt[:, hh, g * D:(g + 1) * D], hs, start=False, stop=True)\
                            .then_inc(g_mm, 1)
                    mm(ps[:, 7, :], wt[:, hh, 2 * D:3 * D], hs, start=True, stop=True).then_inc(g_mm, 1)
                else:
                    mm(ps[:, 4, :], wt[:, ih, 2 * D:3 * D], sup, start=True, stop=True).then_inc(g_mm, 1)

            def out_transpose(f):
                pe.wait_ge(o_sum, f + 1)
                for k in range(KT):
                    last = transpose(ps[:, 5, k * P:(k + 1) * P], gru[:, ST, k * P:(k + 1) * P], ident[:, :])
                last.then_inc(o_t, 1)

            def gru_step(f, j):
                if j == 1:
                    gates(f, 0, 0)
                    gates(f, 0, 1)
                if j == 5:
                    gates(f, 1, 0)
                    gates(f, 1, 1)
                if j == 10:
                    out_transpose(f)

            def layer1(b, first, last_):
                for j in range(NT):
                    if j + 1 < NT:
                        att_chunk(b, j + 1)
                    elif not last_:
                        att_chunk(b + 1, 0)
                    supports(b, j, first)
                    if not first:
                        gru_step(b - 1, j)
                    if not last_ and j == 14:
                        broadcast(b + 1)

            pe.wait_ge(e_rowv, H * NB // 2)
            pe.wait_ge(flag_set, 1)
            att_chunk(0, 0)
            broadcast(0)
            layer1(0, True, False)
            with nc.tensor.Fori(1, NB - 1) as b:
                layer1(b, False, False)
            layer1(NB - 1, False, True)
            for j in range(NT):
                gru_step(NB - 1, j)

            def turn(at, steps, name):
                pe.wait_ge(general_step, at + steps.index(name))

            def product(at, steps, tag, rows, bank, moving, first=True, last=True):
                for q in range(NB):
                    turn(at, steps, f"{tag} transpose {q}")
                    for k in range(KT):
                        done = transpose(ps[:, 0, k * P:(k + 1) * P],
                                         rows[:, (KT * q + k) * P:(KT * q + k + 1) * P], ident[:, :])
                    done.then_inc(general_step, 1)
                    turn(at, steps, f"{tag} multiply {q}")
                    for k in range(KT):
                        j = KT * q + k
                        done = mm(bank, quad[:, k * P:(k + 1) * P], moving(j),
                                  start=(first and j == 0), stop=(last and j == NT - 1))
                    done.then_inc(general_step, 1)

            def transpose_z(at, steps):
                turn(at, steps, "transpose z")
                transpose(ps[:, 0, 0:P], z, ident[:, :]).then_inc(general_step, 1)

            pe.wait_ge(flag_set, 1)
            signed = nc.tensor.value_load(flag[0:1, 0:1], min_val=0, max_val=1)
            with nc.tensor.If(signed != 0):
                with nc.tensor.Fori(0, NT) as t:
                    at = len(MESSAGES) * t + S1
                    transpose_z(at, MESSAGES)
                    turn(at, MESSAGES, "times w0")
                    mm(ps[:, 1, 0:D], zt_g, w0s[:, :], start=True, stop=True).then_inc(general_step, 1)
                with nc.tensor.Fori(0, NT) as t:
                    at = len(WEIGHTS) * t + S2
                    product(at, WEIGHTS, "sum", w_row, ps[:, 1, 0:D], lambda j: g_msg[:, j, :])
                    transpose_z(at, WEIGHTS)
                    turn(at, WEIGHTS, "times W")
                    mm(ps[:, 1, 0:HWC], zt_g, wcat[:, :], start=True, stop=True).then_inc(general_step, 1)
                with nc.tensor.Fori(0, NT) as t:
                    at = len(NEIGHBOURS) * t + S3
                    product(at, NEIGHBOURS, "plus", pos, ps[:, 1, 0:2 * H], lambda j: hw[:, j, H * D:HWC])
                    product(at, NEIGHBOURS, "minus", neg, ps[:, 2, 0:2 * H], lambda j: hw[:, j, H * D:HWC])
                with nc.tensor.Fori(0, NT) as t:
                    turn(len(SPREAD) * t + S4, SPREAD, "spread")
                    for s in range(2):
                        done = mm(ps[:, 1 + s, 0:H * P], ones[:, :], dg6[:, H * s:H * s + H, :]
                                  .rearrange("p h c -> p (h c)"), start=True, stop=True)
                    done.then_inc(general_step, 1)
                with nc.tensor.Fori(0, NT) as t:
                    at = len(ATTEND) * t + S5
                    product(at, ATTEND, "node", a_row, ps[:, 1, 0:D], lambda j: h2[:, j, :])
                    for h in range(H):
                        product(at, ATTEND, f"{h} edge", w_row, ps[:, 2, 0:D],
                                lambda j: hw[:, j, h * D:(h + 1) * D], first=(h == 0), last=(h == H - 1))
                    turn(at, ATTEND, "transpose supports")
                    for s in range(2):
                        done = transpose(ps[:, 0, s * P:(s + 1) * P], sup_rows[:, s, :], ident[:, :])
                    done.then_inc(general_step, 1)
                    hs = h2t[:, bass.ts(t, P)]
                    for c in range(2):
                        turn(at, ATTEND, f"{c} gates")
                        for g in range(2):
                            mm(ps[:, 3 + g, 0:P], wt[:, 2 * c, g * D:(g + 1) * D], sup2[:, c, :],
                               start=True, stop=False)
                            mm(ps[:, 3 + g, 0:P], wt[:, 2 * c + 1, g * D:(g + 1) * D], hs,
                               start=False, stop=True)
                        mm(ps[:, 5, 0:P], wt[:, 2 * c + 1, 2 * D:3 * D], hs, start=True, stop=True)
                        mm(ps[:, 6, 0:P], wt[:, 2 * c, 2 * D:3 * D], sup2[:, c, :], start=True, stop=True)\
                            .then_inc(general_step, 1)
                    turn(at, ATTEND, "transpose out")
                    transpose(ps[:, 0, 0:P], g_sum, ident[:, :]).then_inc(general_step, 1)

        @block.scalar
        def _(act):
            activation = nc.scalar.activation

            act.preload_act_table_set("natural_log_exp_and_others")
            act.wait_ge(const_set, 9)
            act.wait_ge(p_stat, 1)
            activation(rstd[:, :], mv[:, :, 1], ACT.Ln, bias=epsb[:, :]).then_inc(recip_ln0, 1)
            act.wait_ge(recip_ln0, 1)
            activation(rstd[:, :], rstd[:, :], ACT.Exp, scale=-0.5).then_inc(p_rstd, 1)
            act.wait_ge(wprep, 1)
            activation(stage, ps[:, 7, 0:H * D], ACT.Copy).then_inc(wcopied, 1)
            act.wait_ge(wprep, 2)
            activation(wcat[:, H * D:HWC], ps[:, 6, 0:2 * H], ACT.Copy).then_inc(wcopied, 1)
            for g in range(NB):
                act.wait_ge(p_zt, g + 1)
                if g:
                    act.wait_ge(p_msg, g)
                activation(zt, ps[:, 5, :], ACT.Copy).then_inc(p_ztc, 1)

            def reciprocal(b, j):
                u = NT * b + j
                act.wait_ge(adj_t, u + 1)
                if not (isinstance(b, int) and b == 0 and j < 4):
                    act.wait_ge(sq_done, u - 3)
                activation(rec[:, j % 4, :], ps[:, j % 4, :], ACT.Ln, bias=tinyb[:, :]).then_inc(ln_adj, 1)
                act.wait_ge(ln_adj, u + 1)
                activation(rec[:, j % 4, :], rec[:, j % 4, :], ACT.Exp, scale=-1.0).then_inc(recip, 1)

            def sensitivity(b, j):
                act.wait_ge(sq_done, NT * b + j + 1)
                activation(wgt[:, j % 4, :], wgt[:, j % 4, :], ACT.Exp, bias=two[:, :], scale=-2.0)\
                    .then_inc(sens, 1)

            def finish(f, step):
                if step == 3:
                    act.wait_ge(summed, NT * f + NT)
                    activation(xs, ps[:, 4, :], ACT.Copy).then_inc(f_xs, 1)
                if step == 5:
                    act.wait_ge(f_stat, f + 1)
                    activation(rstd[:, 0:KT], mv[:, 0:KT, 1], ACT.Ln, bias=epsb[:, :]).then_inc(f_ln, 1)
                    act.wait_ge(f_ln, f + 1)
                    activation(rstd[:, 0:KT], rstd[:, 0:KT], ACT.Exp, scale=-0.5).then_inc(f_rstd, 1)
                if step == 8:
                    act.wait_ge(f_zt, f + 1)
                    act.wait_ge(f_keep, 2 * f + 2)
                    activation(zt, ps[:, 6, :], ACT.Copy).then_inc(f_ztc, 1)
                if step in (10, 12):
                    k = step - 10
                    act.wait_ge(f_hw, KT * f + k + 1)
                    activation(hw[:, bass.ds(KT * f + k, 1), :], ps[:, 7:8, 0:HWC], ACT.Copy).then_inc(f_hwa, 1)

            def layer0(b, first):
                for j in range(NT):
                    if not first:
                        finish(b - 1, j)
                    reciprocal(b, j)
                    if j:
                        sensitivity(b, j - 1)
                    elif not first:
                        sensitivity(b - 1, NT - 1)

            layer0(0, True)
            with nc.scalar.Fori(1, NB) as b:
                layer0(b, False)
            sensitivity(NB - 1, NT - 1)
            for step in range(NT):
                finish(NB - 1, step)
                if step == 3:
                    for c in range(4):
                        act.wait_ge(wprep, 3 + c)
                        activation(wt[:, c, :], ps[:, c, 0:NG], ACT.Copy).then_inc(wcopied, 1)

            def copy_row(n):
                act.wait_ge(e_row, n + 1)
                activation(neb[:, n // NB, (n % NB) * BLK:(n % NB + 1) * BLK], ps[:, 1 + n % 4, :],
                           ACT.Copy).then_inc(e_rowa, 1)

            def denominator(s, n):
                act.wait_ge(max_done, KT * H * s + n + 1)
                view = sc[:, n % 2, :]
                activation(view, view, ACT.Sigmoid, bias=negmc[:, n:n + 1], scale=-1.0,
                           accum_out=den[:, n:n + 1]).then_inc(den_done, 1)

            def logarithms(s):
                act.wait_ge(den_done, KT * H * s + KT * H)
                activation(den[:, :], den[:, :], ACT.Ln, scale=H * math.exp(2 * C)).then_inc(ln_done, 1)

            def copy_nml(s):
                for h in range(H):
                    act.wait_ge(bc_done, H * s + h + 1)
                    if h == 0 and not (isinstance(s, int) and s == 0):
                        act.wait_ge(t_done, H * NT * s)
                    activation(nmb[:, h, :], ps[:, 4 + h, :], ACT.Copy).then_inc(nmb_done, 1)

            def copy_att(b, j):
                u = NT * b + j
                act.wait_ge(att_t, u + 1)
                if not (isinstance(b, int) and b == 0 and j < 2):
                    act.wait_ge(u_done, H * u - H)
                    act.wait_ge(ns_mm, u - 1)
                activation(att[:, j % 2, :], ps[:, j % 2, :], ACT.Copy).then_inc(att_done, 1)

            def attention(b, j):
                for h in range(H):
                    n = H * j + h
                    if j == 0:
                        act.wait_ge(nmb_done, H * b + h + 1)
                    if not (isinstance(b, int) and b == 0 and n < 4):
                        act.wait_ge(u_done, H * NT * b + n - 3)
                    activation(tt[:, n % 4, :], nmb[:, h, :], ACT.Sigmoid, bias=ew[:, h, j:j + 1])\
                        .then_inc(t_done, 1)

            def gru_step(f, j):
                if j == 1:
                    act.wait_ge(ns_mm, NT * f + NT)
                    activation(gru[:, NSB, :], ps[:, 2, :], ACT.Copy).then_inc(sup_out, 1)
                    act.wait_ge(es_mm, H * NT * f + H * NT)
                    activation(gru[:, ESB, :], ps[:, 3, :], ACT.Copy, scale=math.exp(C)).then_inc(sup_out, 1)
                if j in (2, 6):
                    c = j // 5
                    act.wait_ge(g_mm, 8 * f + 4 * c + 2)
                    if c:
                        act.wait_ge(vg, OWN * f + CELL)
                    activation(gru[:, TR, :], ps[:, 5, :], ACT.Sigmoid, bias=gb[:, c, 0:1])\
                        .then_inc(g_act, 1)
                    activation(gru[:, TZ, :], ps[:, 6, :], ACT.Sigmoid, bias=gb[:, c, 1:2])\
                        .then_inc(g_act, 1)
                if j in (5, 9):
                    c = j // 9
                    act.wait_ge(g_dve, 4 * f + 2 * c + 2)
                    activation(gru[:, NN, :], gru[:, UV, :], ACT.Tanh, bias=bi[:, 2 * c, 2:3])\
                        .then_inc(g_act, 1)

            def layer1(b, first, last_):
                for j in range(NT):
                    if not first:
                        gru_step(b - 1, j)
                    copy_att(b, j)
                    attention(b, j)
                    if not last_ and 0 < j <= KT * H:
                        denominator(b + 1, j - 1)
                    if not last_ and j == KT * H:
                        logarithms(b + 1)
                if not last_:
                    copy_nml(b + 1)

            act.preload_act_table_set("sigmoid_and_others")
            for n in range(KT * H):
                if n < H:
                    copy_row(NB * n)
                    copy_row(NB * n + 2)
                if n:
                    denominator(0, n - 1)
            denominator(0, KT * H - 1)
            logarithms(0)
            copy_nml(0)
            layer1(0, True, False)
            with nc.scalar.Fori(1, NB - 1) as b:
                layer1(b, False, False)
            layer1(NB - 1, False, True)
            for j in range(NT):
                gru_step(NB - 1, j)

            def general(at, steps, name, *args, **kwargs):
                act.wait_ge(general_step, at + steps.index(name))
                activation(*args, **kwargs).then_inc(general_step, 1)

            def inverse_deviation(at, steps):
                general(at, steps, "ln", rstd[:, 0:1], mv[:, 0, 1:2], ACT.Ln, bias=epsb[:, :])
                general(at, steps, "rsqrt", rstd[:, 0:1], rstd[:, 0:1], ACT.Exp, scale=-0.5)

            act.wait_ge(flag_set, 1)
            signed = nc.scalar.value_load(flag[0:1, 0:1], min_val=0, max_val=1)
            with nc.scalar.If(signed != 0):
                with nc.scalar.Fori(0, NT) as t:
                    inverse_deviation(len(MESSAGES) * t + S1, MESSAGES)
                with nc.scalar.Fori(0, NT) as t:
                    at = len(WEIGHTS) * t + S2
                    general(at, WEIGHTS, "exp", w_row, w_row, ACT.Exp, bias=two[:, :], scale=-2.0)
                    inverse_deviation(at, WEIGHTS)
                with nc.scalar.Fori(0, NT) as t:
                    at = len(ATTEND) * t + S5
                    for h in range(H):
                        general(at, ATTEND, f"{h} exp", score, score, ACT.Sigmoid,
                                bias=g_small[:, G_BIAS:G_BIAS + 1])
                    for c in range(2):
                        general(at, ATTEND, f"{c} sigmoid r", g_r, ps[:, 3, 0:P], ACT.Sigmoid,
                                bias=gb[:, c, 0:1])
                        general(at, ATTEND, f"{c} sigmoid z", g_z, ps[:, 4, 0:P], ACT.Sigmoid,
                                bias=gb[:, c, 1:2])
                        general(at, ATTEND, f"{c} tanh", g_n, g_r, ACT.Tanh, bias=bi[:, 2 * c, 2:3])

        @block.vector
        def _(dve):
            v = nc.vector

            held = [0]

            def hold(b):
                if not isinstance(b, int):
                    held[0] = (held[0] + 1) % 16
                    v.memset(unused[:, held[0]:held[0] + 1], 0.0)

            def chain(semaphore, count):
                made = [count]

                def step(ins):
                    made[0] = made[0] + 1
                    ins.then_inc(semaphore, 1)
                    dve.wait_ge(semaphore, made[0])
                return step

            def refine(step, r, m):
                w_ = nwt[:, 0:r.shape[1]]
                step(v.scalar_tensor_tensor(w_, m, EPS, r, ALU.add, ALU.mult))
                step(v.tensor_tensor(w_, w_, r, ALU.mult))
                step(v.tensor_scalar(w_, w_, -0.5, 1.5, ALU.mult, ALU.add))
                step(v.tensor_tensor(r, r, w_, ALU.mult))

            def add_bias(g):
                dve.wait_ge(p_msg, g + 1)
                v.tensor_tensor(msg[:, KT * g:KT * g + KT, :],
                                ps[:, 4, :].rearrange("p (k d) -> p k d", k=KT),
                                b0s[:, :].rearrange("p (o d) -> p o d", o=1).broadcast_to([P, KT, D]),
                                ALU.add).then_inc(p_msgc, 1)

            dve.wait_ge(x_in, 16)
            for t in range(NT):
                last = v.bn_stats(stat[:, t, :], xb[:, t, :])
            pro = chain(vp, 0)
            pro(last)
            for t in range(NT):
                last = v.bn_aggr(mv[:, t, :], stat[:, t, :])
            last.then_inc(p_stat, 1)
            dve.wait_ge(p_rstd, 1)
            refine(pro, rstd[:, :], mv[:, :, 1])
            for g in range(NB):
                if g:
                    dve.wait_ge(p_zt, g)
                for k in range(KT):
                    t = KT * g + k
                    last = v.tensor_scalar(zr[:, k, :], xb[:, t, :], mv[:, t, 0:1], rstd[:, t:t + 1],
                                           ALU.subtract, ALU.mult)
                pro(last)
                v.tensor_scalar(zr, zr, 0.0, None, ALU.max).then_inc(p_z, 1)
                if g:
                    add_bias(g - 1)
            add_bias(NB - 1)
            dve.wait_ge(diag_in, 80)
            for c in range(2):
                pro(v.tensor_tensor(gb[:, c, :], bi[:, 2 * c, 0:2], bi[:, 2 * c + 1, 0:2], ALU.add))

            def squared(b, j):
                u = NT * b + j
                dve.wait_ge(recip, u + 1)
                if not (isinstance(b, int) and b == 0 and j < 4):
                    dve.wait_ge(mask_kept, u - 3)
                hold(b)
                v.tensor_scalar(mstage[:, j % 4, :], ps[:, j % 4, :], HUGE, 1.0, ALU.mult, ALU.min,
                                saturate=False).then_inc(mask_done, 1)
                if not (isinstance(b, int) and b == 0 and j < 4):
                    dve.wait_ge(summed, u - 3)
                r = rec[:, j % 4, :]
                v.scalar_tensor_tensor(wgt[:, j % 4, :], r, -2.0, r, ALU.add, ALU.mult).then_inc(sq_done, 1)

            def weigh(b, j):
                dve.wait_ge(sens, NT * b + j + 1)
                w_ = wgt[:, j % 4, :]
                v.scalar_tensor_tensor(w_, ps[:, j % 4, :], 1.0, w_, ALU.is_lt, ALU.mult).then_inc(wgt_done, 1)

            FIN = 8

            def finish(f, step):
                if step == 4:
                    dve.wait_ge(f_xt, f + 1)
                    fin = chain(vf, FIN * f)
                    dve.wait_ge(f_keep, 2 * f + 1)
                    rows = xb[:, bass.ts(f, KT), :]
                    fin(v.tensor_tensor(zr, ps[:, 5, :].rearrange("p (k d) -> p k d", k=KT), rows, ALU.add))
                    hold(f)
                    fin(v.tensor_copy(rows, zr))
                    for k in range(KT):
                        last = v.bn_stats(stat[:, k, :], zr[:, k, :])
                    fin(last)
                    hold(f)
                    for k in range(KT):
                        last = v.bn_aggr(mv[:, k, :], stat[:, k, :])
                    last.then_inc(f_stat, 1)
                if step == 6:
                    dve.wait_ge(f_rstd, f + 1)
                    fin = chain(vf, FIN * f + 3)
                    refine(fin, rstd[:, 0:KT], mv[:, 0:KT, 1])
                    for k in range(KT):
                        last = v.tensor_scalar(zr[:, k, :], zr[:, k, :], mv[:, k, 0:1],
                                               rstd[:, k:k + 1], ALU.subtract, ALU.mult)
                    fin(last)
                    v.tensor_scalar(zr, zr, 0.0, None, ALU.max).then_inc(f_z, 1)
                if step in (10, 12):
                    k = step - 9
                    dve.wait_ge(f_hw, KT * f + k + 1)
                    v.tensor_copy(hw[:, bass.ds(KT * f + k, 1), :], ps[:, (7, 5, 7, 6)[k]:(7, 5, 7, 6)[k] + 1, 0:HWC])\
                        .then_inc(f_hwv, 1)

            def layer0(b, first):
                for j in range(NT):
                    if j >= 1:
                        squared(b, j - 1)
                    elif not first:
                        squared(b - 1, NT - 1)
                    if j >= 2:
                        weigh(b, j - 2)
                    elif not first:
                        weigh(b - 1, NT - 2 + j)
                    if not first:
                        finish(b - 1, j)

            layer0(0, True)
            with nc.vector.Fori(1, NB) as b:
                layer0(b, False)
            squared(NB - 1, NT - 1)
            weigh(NB - 1, NT - 2)
            weigh(NB - 1, NT - 1)
            for step in range(NT):
                finish(NB - 1, step)

            tr = chain(vt, 0)
            dve.wait_ge(f_hwa, NT // 2)
            dve.wait_ge(f_hwv, NT // 2)
            hu = hw[:, :, H * D:H * D + 2 * H].rearrange("p t (h s) -> p t h s", s=2)[:, :, :, 0]
            tr(v.tensor_copy(hu3[:, :, 0:H], hu))
            tr(v.tensor_tensor(hur[:, 0], hu, hu3[:, :, 0:H], ALU.subtract))
            tr(v.tensor_copy(hu3[:, :, H:2 * H], hur[:, 0]))
            tr(v.tensor_tensor(hur[:, 1], hur[:, 0], hu3[:, :, H:2 * H], ALU.subtract))
            v.tensor_copy(hu3[:, :, 2 * H:3 * H], hur[:, 1]).then_inc(hu_split, 1)

            dve.wait_ge(q_done, 1)
            sums = ps[:, 0, 0:NT * HC].rearrange("p (t c) -> p t c", t=NT)
            tr(v.tensor_reduce(qs[:, :, :], sums[:, :, 0:3 * H].rearrange("p t (s h) -> p t h s", s=3),
                               AX.X, ALU.add))
            v.scalar_tensor_tensor(ew[:, :, :], qs[:, :, :].rearrange("p t h -> p h t"), 0.2,
                                   qs[:, :, :].rearrange("p t h -> p h t"), ALU.mult, ALU.max).then_inc(e_done, 1)
            dve.wait_ge(e_done, 1)
            v.tensor_scalar(nege[:, :, :], ew[:, :, :], -1.0, None, ALU.mult).then_inc(e_done, 1)
            v.tensor_scalar(okc[:, 0, :], sums[:, :, 3 * H], 0.0, None, ALU.is_ge)
            tr(v.tensor_scalar(okc[:, 1, :], de[:, :], 0.0, None, ALU.is_ge))
            v.tensor_reduce(okm[:, 0:1], okc[:, :, :], AX.XY, ALU.min).then_inc(ok_min, 1)

            def copy_row(n):
                dve.wait_ge(e_row, n + 1)
                v.tensor_copy(neb[:, n // NB, (n % NB) * BLK:(n % NB + 1) * BLK], ps[:, 1 + n % 4, :])\
                    .then_inc(e_rowv, 1)

            def spread(m):
                return m.rearrange("p (o c) -> p o c", o=1)

            def set_flag():
                dve.wait_ge(ok_t, 1)
                tr(v.tensor_reduce(okm[0:1, 1:2], ps[0:1, 0, 256:256 + P], AX.X, ALU.min))
                v.tensor_scalar(flag[:, :], okm[0:1, 1:2], 0.5, None, ALU.is_lt).then_inc(flag_set, 1)

            def scores(s, n):
                t, h = KT * s + n // H, n % H
                if n % H == 0 and isinstance(s, int) and s == 0:
                    dve.wait_ge(*((pen_done, t + 1) if t < 2 else (pen_own, t - 1)))
                elif n % H == 0:
                    dve.wait_ge(pen_done, t - 1)
                if not (isinstance(s, int) and s == 0 and n < 2):
                    dve.wait_ge(den_done, KT * H * s + n - 1)
                hold(s)
                v.tensor_tensor_reduce(out=sc[:, n % 2, :], in0=pen[:, (n // H) % 2, :], in1=neb[:, h, :],
                                       scale=1.0, scalar=3.0e38, op0=ALU.add, op1=ALU.min,
                                       accum_out=negm[:, n:n + 1]).then_inc(sc_done, 1)

            def maximum(s, n):
                dve.wait_ge(sc_done, KT * H * s + n + 1)
                v.tensor_scalar(negmc[:, n:n + 1], negm[:, n:n + 1], -C, None, ALU.add).then_inc(max_done, 1)

            def logarithm_sum(s):
                dve.wait_ge(ln_done, s + 1)
                if not (isinstance(s, int) and s == 0):
                    dve.wait_ge(bc_done, H * s)
                v.tensor_tensor(nml[:, :], negm[:, :], den[:, :], ALU.subtract).then_inc(nml_done, 1)
                dve.wait_ge(nml_done, s + 1)

            def attend(b, j):
                dve.wait_ge(att_done, NT * b + j + 1)
                for h in range(H):
                    n = H * j + h
                    dve.wait_ge(t_done, H * NT * b + n + 1)
                    if not (isinstance(b, int) and b == 0 and n < 4):
                        dve.wait_ge(es_mm, H * NT * b + n - 3)
                    v.tensor_tensor(uu[:, n % 4, :], tt[:, n % 4, :], att[:, j % 2, :],
                                    ALU.mult).then_inc(u_done, 1)

            def gru_step(f, j):
                if j in (3, 7):
                    c = j // 7
                    dve.wait_ge(g_act, 6 * f + 3 * c + 1)
                    dve.wait_ge(g_mm, 8 * f + 4 * c + 3)
                    v.scalar_tensor_tensor(gru[:, UV, :], ps[:, 7, :], bi[:, 2 * c + 1, 2:3], gru[:, TR, :],
                                           ALU.add, ALU.mult).then_inc(g_dve, 1)
                if j in (4, 8):
                    c = j // 8
                    dve.wait_ge(g_mm, 8 * f + 4 * c + 4)
                    dve.wait_ge(g_dve, 4 * f + 2 * c + 1)
                    v.tensor_tensor(gru[:, UV, :], gru[:, UV, :], ps[:, 4, :], ALU.add).then_inc(g_dve, 1)
                if j in (5, 9):
                    c = j // 9
                    own = chain(vg, OWN * f + CELL * c)
                    dve.wait_ge(g_act, 6 * f + 3 * c + 3)
                    own(v.tensor_tensor(gru[:, DD, :], h2t[:, bass.ts(f, BLK)], gru[:, NN, :], ALU.subtract))
                    own(v.tensor_tensor(gru[:, DD, :], gru[:, TZ, :], gru[:, DD, :], ALU.mult))
                    own(v.tensor_tensor(gru[:, OE if c == 0 else ST, :], gru[:, DD, :], gru[:, NN, :], ALU.add))
                if j == 10:
                    dve.wait_ge(vg, OWN * f + OWN)
                    v.tensor_tensor(gru[:, ST, :], gru[:, ST, :], gru[:, OE, :], ALU.add).then_inc(o_sum, 1)
                if j == 11:
                    dve.wait_ge(o_t, f + 1)
                    dve.wait_ge(stored, 16 * f + 16)
                    for k in range(KT):
                        last = v.scalar_tensor_tensor(osb[:, k:k + 1, :], ps[:, 5:6, k * D:(k + 1) * D],
                                                      de[:, bass.ds(KT * f + k, 1)],
                                                      xb[:, bass.ds(KT * f + k, 1), :], ALU.mult, ALU.add)
                    last.then_inc(o_done, 1)

            def layer1(b, first, last_):
                for j in range(NT):
                    if not last_ and j < KT * H:
                        scores(b + 1, j)
                    attend(b, j)
                    if not last_ and j < KT * H:
                        maximum(b + 1, j)
                    if not first:
                        gru_step(b - 1, j)
                    if not last_ and j == 13:
                        logarithm_sum(b + 1)

            def own_pen(t):
                dve.wait_ge(row_in[t % 2], 32)
                dve.wait_ge(sc_done, H * (t - 1))
                tr(v.tensor_scalar(pen[:, t % 2, :], row[:, t % 2, :], 0.0, OUT, ALU.is_le, ALU.mult))
                spot = pen[:, t % 2, P * t:P * t + P]
                v.tensor_tensor(spot, spot, outdiag[:, :], ALU.max).then_inc(pen_own, 1)

            for n in range(KT * H):
                if n < H:
                    copy_row(NB * n + 1)
                    copy_row(NB * n + 3)
                    dve.wait_ge(e_rowa, 2 * n + 2)
                    dve.wait_ge(e_rowv, 2 * n + 2)
                if n in (H, 2 * H):
                    own_pen(n // H + 1)
                scores(0, n)
                maximum(0, n)
                if n == H:
                    set_flag()
            logarithm_sum(0)
            layer1(0, True, False)
            with nc.vector.Fori(1, NB - 1) as b:
                layer1(b, False, False)
            layer1(NB - 1, False, True)
            for j in range(NT):
                gru_step(NB - 1, j)

            def turn(at, steps, name):
                dve.wait_ge(general_step, at + steps.index(name))

            def done(ins):
                ins.then_inc(general_step, 1)

            def copies(at, steps, tag):
                for q in range(NB):
                    turn(at, steps, f"{tag} copy {q}")
                    done(v.tensor_copy(quad, ps[:, 0, :]))

            def normalise(at, steps):
                turn(at, steps, "stats")
                done(v.bn_stats(stat[:, 0, :], cur))
                turn(at, steps, "aggregate")
                hold(at)
                done(v.bn_aggr(mv[:, 0, :], stat[:, 0, :]))
                r, w_ = rstd[:, 0:1], nwt[:, 0:1]
                turn(at, steps, "newton 0")
                done(v.scalar_tensor_tensor(w_, mv[:, 0, 1:2], EPS, r, ALU.add, ALU.mult))
                turn(at, steps, "newton 1")
                done(v.tensor_tensor(w_, w_, r, ALU.mult))
                turn(at, steps, "newton 2")
                done(v.tensor_scalar(w_, w_, -0.5, 1.5, ALU.mult, ALU.add))
                turn(at, steps, "newton 3")
                done(v.tensor_tensor(r, r, w_, ALU.mult))
                turn(at, steps, "normalise")
                done(v.tensor_scalar(z, cur, mv[:, 0, 0:1], r, ALU.subtract, ALU.mult))
                turn(at, steps, "relu")
                done(v.tensor_scalar(z, z, 0.0, None, ALU.max))
                turn(at, steps, "copy z")
                done(v.tensor_copy(zt_g, ps[:, 0, 0:P]))

            def signs(at, steps, t):
                turn(at, steps, "no diagonal")
                spot = a_row[:, bass.ts(t, P)]
                done(v.tensor_tensor(spot, spot, offdiag[:, :], ALU.mult))
                turn(at, steps, "pos")
                done(v.tensor_scalar(pos, a_row, 0.0, None, ALU.is_gt))
                turn(at, steps, "neg")
                done(v.tensor_scalar(neg, a_row, 0.0, None, ALU.is_lt))

            signed = nc.vector.value_load(flag[0:1, 0:1], min_val=0, max_val=1)
            with nc.vector.If(signed != 0):
                dve.wait_ge(g_x_in, 16)
                with nc.vector.Fori(0, NT) as t:
                    at = len(MESSAGES) * t + S1
                    turn(at, MESSAGES, "fetch")
                    done(v.tensor_scalar(cur, xb[:, bass.ds(t, 1), :].rearrange("p o d -> p (o d)"),
                                         0.0, None, ALU.add))
                    normalise(at, MESSAGES)
                    turn(at, MESSAGES, "add b0")
                    done(v.tensor_tensor(g_msg[:, bass.ds(t, 1), :], ps[:, 1:2, 0:D],
                                         b0s[:, :].rearrange("p (o d) -> p o d", o=1), ALU.add))

                SMALL = 2.0 ** -40
                with nc.vector.Fori(0, NT) as t:
                    at = len(WEIGHTS) * t + S2
                    turn(at, WEIGHTS, "square")
                    dve.wait_ge(g_row_in, 16 * t + 16)
                    done(v.tensor_tensor(pos, a_row, a_row, ALU.mult))
                    turn(at, WEIGHTS, "clamp")
                    done(v.tensor_scalar(pos, pos, SMALL, None, ALU.max))
                    turn(at, WEIGHTS, "reciprocal")
                    done(v.reciprocal(neg, pos))
                    turn(at, WEIGHTS, "r")
                    done(v.tensor_tensor(neg, neg, a_row, ALU.mult))
                    turn(at, WEIGHTS, "q")
                    done(v.scalar_tensor_tensor(w_row, neg, -2.0, neg, ALU.add, ALU.mult))
                    turn(at, WEIGHTS, "below 1")
                    done(v.scalar_tensor_tensor(w_row, a_row, 1.0, w_row, ALU.is_lt, ALU.mult))
                    turn(at, WEIGHTS, "not 0")
                    done(v.scalar_tensor_tensor(w_row, pos, SMALL, w_row, ALU.is_gt, ALU.mult))
                    copies(at, WEIGHTS, "sum")
                    x_rows = xb[:, bass.ds(t, 1), :]
                    turn(at, WEIGHTS, "x1")
                    done(v.tensor_tensor(cur.rearrange("p (o d) -> p o d", o=1), ps[:, 1:2, 0:D],
                                         x_rows, ALU.add))
                    turn(at, WEIGHTS, "keep x1")
                    done(v.tensor_scalar(x_rows.rearrange("p o d -> p (o d)"), cur, 0.0, None, ALU.add))
                    normalise(at, WEIGHTS)
                    turn(at, WEIGHTS, "keep h2")
                    done(v.tensor_scalar(h2[:, bass.ds(t, 1), :].rearrange("p o d -> p (o d)"), z,
                                         0.0, None, ALU.add))
                    turn(at, WEIGHTS, "keep h2t")
                    done(v.tensor_scalar(h2t[:, bass.ts(t, P)], zt_g, 0.0, None, ALU.add))
                    turn(at, WEIGHTS, "keep hw")
                    done(v.tensor_scalar(hw[:, bass.ds(t, 1), :], ps[:, 1:2, 0:HWC], 0.0, None, ALU.add))

                with nc.vector.Fori(0, NT) as t:
                    at = len(NEIGHBOURS) * t + S3
                    dve.wait_ge(g_row_in, 16 * t + 16 * NT + 16)
                    signs(at, NEIGHBOURS, t)
                    copies(at, NEIGHBOURS, "plus")
                    copies(at, NEIGHBOURS, "minus")
                    turn(at, NEIGHBOURS, "keep plus")
                    done(v.tensor_copy(nbr, ps[:, 1, 0:2 * H]))
                    plus = nbr.rearrange("p (h s) -> p h s", s=2)
                    minus = ps[:, 2, 0:2 * H].rearrange("p (h s) -> p h s", s=2)
                    sums = g_sum[:, 0:2 * H]
                    turn(at, NEIGHBOURS, "e_plus")
                    done(v.tensor_tensor(sums[:, 0:H], plus[:, :, 0], minus[:, :, 1], ALU.add))
                    turn(at, NEIGHBOURS, "e_minus")
                    done(v.tensor_tensor(sums[:, H:2 * H], plus[:, :, 1], minus[:, :, 0], ALU.add))
                    for s, name in enumerate(("leaky plus", "leaky minus")):
                        turn(at, NEIGHBOURS, name)
                        part_ = sums[:, H * s:H * s + H].rearrange("p (h o) -> p h o", o=1)
                        done(v.scalar_tensor_tensor(e_col[:, H * s:H * s + H, bass.ds(t, 1)], part_, 0.2,
                                                    part_, ALU.mult, ALU.max))

                with nc.vector.Fori(0, NT) as t:
                    at = len(SPREAD) * t + S4
                    turn(at, SPREAD, "diagonals")
                    done(v.tensor_tensor(dg6, spread(ident[:, :]).broadcast_to([P, 2 * H, P]),
                                         e_col[:, :, bass.ds(t, 1)].broadcast_to([P, 2 * H, P]), ALU.mult))
                    for s, name in enumerate(("copy plus", "copy minus")):
                        turn(at, SPREAD, name)
                        done(v.tensor_scalar(e_all[:, H * s:H * s + H, bass.ts(t, P)],
                                             ps[:, 1 + s, 0:H * P].rearrange("p (h c) -> p h c", h=H),
                                             0.0, None, ALU.add))

                with nc.vector.Fori(0, NT) as t:
                    at = len(ATTEND) * t + S5
                    dve.wait_ge(g_row_in, 16 * t + 32 * NT + 16)
                    signs(at, ATTEND, t)
                    turn(at, ATTEND, "none")
                    done(v.tensor_scalar(none, a_row, 0.0, -9.0e15, ALU.is_equal, ALU.mult))
                    copies(at, ATTEND, "node")
                    for h in range(H):
                        def head(name):
                            turn(at, ATTEND, f"{h} {name}")

                        head("plus score")
                        done(v.tensor_tensor(score, pos, e_all[:, h, :], ALU.mult))
                        head("minus score")
                        done(v.tensor_tensor(score2, neg, e_all[:, H + h, :], ALU.mult))
                        head("both")
                        done(v.tensor_tensor(score, score, score2, ALU.add))
                        head("outside")
                        done(v.tensor_tensor(score, score, none, ALU.add))
                        head("max")
                        done(v.tensor_reduce(g_small[:, G_MAX:G_MAX + 1], score, AX.X, ALU.max))
                        head("bias")
                        done(v.tensor_scalar(g_small[:, G_BIAS:G_BIAS + 1], g_small[:, G_MAX:G_MAX + 1],
                                             -1.0, -C, ALU.mult, ALU.add))
                        head("denominator")
                        done(v.tensor_reduce(g_small[:, G_DEN:G_DEN + 1], score, AX.X, ALU.add))
                        head("reciprocal")
                        done(v.reciprocal(g_small[:, G_RDEN:G_RDEN + 1], g_small[:, G_DEN:G_DEN + 1]))
                        head("probability")
                        done(v.scalar_tensor_tensor(w_row, score, g_small[:, G_RDEN:G_RDEN + 1], a_row,
                                                    ALU.mult, ALU.mult))
                        copies(at, ATTEND, f"{h} edge")
                    for s, name in enumerate(("keep node", "keep edge")):
                        turn(at, ATTEND, name)
                        done(v.tensor_scalar(sup_rows[:, s, :], ps[:, 1 + s, 0:D], (1.0, 1.0 / H)[s], None,
                                             ALU.mult))
                    turn(at, ATTEND, "copy supports")
                    done(v.tensor_copy(sup2, ps[:, 0, 0:2 * P].rearrange("p (s c) -> p s c", s=2)))
                    for c in range(2):
                        def cell(name):
                            turn(at, ATTEND, f"{c} {name}")

                        cell("times r")
                        done(v.scalar_tensor_tensor(g_r, ps[:, 5, 0:P], bi[:, 2 * c + 1, 2:3], g_r,
                                                    ALU.add, ALU.mult))
                        cell("add in")
                        done(v.tensor_tensor(g_r, g_r, ps[:, 6, 0:P], ALU.add))
                        cell("h - n")
                        done(v.tensor_tensor(g_d, h2t[:, bass.ts(t, P)], g_n, ALU.subtract))
                        cell("times z")
                        done(v.tensor_tensor(g_d, g_d, g_z, ALU.mult))
                        cell("add n")
                        done(v.tensor_tensor(g_out if c == 0 else g_sum, g_d, g_n, ALU.add))
                    turn(at, ATTEND, "add cells")
                    done(v.tensor_tensor(g_sum, g_sum, g_out, ALU.add))
                    turn(at, ATTEND, "out")
                    done(v.scalar_tensor_tensor(g_out.rearrange("p (o d) -> p o d", o=1), ps[:, 0:1, 0:P],
                                                de[:, bass.ds(t, 1)], xb[:, bass.ds(t, 1), :],
                                                ALU.mult, ALU.add))


_INS = ["x", "adj", "L0_gnn_W", "L0_gnn_B", "L1_gnn_gat_W", "L1_gnn_gat_a",
        "L1_gnn_edge_Wih", "L1_gnn_edge_Whh", "L1_gnn_edge_bih", "L1_gnn_edge_bhh",
        "L1_gnn_node_Wih", "L1_gnn_node_Whh", "L1_gnn_node_bih", "L1_gnn_node_bhh"]


def kernel(**inputs):
    import concourse.bacc as _bacc
    from concourse.bass_utils import run_bass_kernel_spmd as _run

    nc = _bacc.Bacc("TRN2", target_bir_lowering=False, num_devices=1)
    arrays, args = {}, []
    for name in _INS:
        a = np.ascontiguousarray(inputs[name])
        arrays[f"in_{name}"] = a
        args.append(nc.dram_tensor(f"in_{name}", a.shape, mybir.dt.from_np(a.dtype), kind="ExternalInput").ap())
    args.append(nc.dram_tensor("out_x", (N, D), F32, kind="ExternalOutput").ap())
    program(nc, *args)
    r = _run(nc, [arrays], core_ids=[0])
    return r.results[0]["out_x"]
```

```python
import math
from contextlib import ExitStack

import numpy as np
import concourse.bass as bass
from concourse import mybir

F32 = mybir.dt.float32
BF16 = mybir.dt.bfloat16
F8 = mybir.dt.float8e5
I32 = mybir.dt.int32
ALU = mybir.AluOpType
ACT = mybir.ActivationFunctionType
AX = mybir.AxisListType

N, D, H, P = 2048, 128, 3, 128
NT = N // P
BLK = 512
NB = N // BLK
KT = BLK // P
NG = 3 * D
UU = 6
HWC = H * D + 2 * H
HC = 3 * H + 1
EPS = 1e-5
TINY = 2.0 ** -60
HUGE = 2.0 ** 127
C = 17.375
OUT = 2.0 ** 100


def program(nc, x, adj, w0, b0, gat_w, gat_a, e_wih, e_whh, e_bih, e_bhh,
            n_wih, n_whh, n_bih, n_bhh, out):
    ctx = ExitStack()
    with ctx:
        def sb(name, shape, dt=F32):
            return ctx.enter_context(nc.sbuf_tensor(name, shape, dt))

        def sem(name):
            return ctx.enter_context(nc.semaphore(name))

        xb = sb("xb", [P, NT, D])
        h2 = sb("h2", [P, NT, D])
        h2t = sb("h2t", [P, N])
        hw = sb("hw", [P, NT, HWC])
        col = sb("col", [P, NB, KT, BLK])
        row = sb("row", [P, 2, N])
        pen = sb("pen", [P, 2, N], BF16)
        sc = sb("sc", [P, 2, N])
        ident = sb("ident", [P, P])
        ones = sb("ones", [P, P])
        offdiag = sb("offdiag", [P, P], BF16)
        outdiag = sb("outdiag", [P, P], BF16)
        wcat = sb("wcat", [P, HWC])
        w0s = sb("w0s", [P, D])
        b0s = sb("b0s", [P, D])
        gas = sb("gas", [P, H, 2])
        de = sb("de", [P, NT])
        wt = sb("wt", [P, 4, NG])
        bi = sb("bi", [P, 4, 3])
        gb = sb("gb", [P, 2, 2])
        stat = sb("stat", [P, NT, 6])
        mv = sb("mv", [P, NT, 2])
        var = sb("var", [P, NT])
        rstd = sb("rstd", [P, NT])
        nwt = sb("nwt", [P, NT])
        hu3 = sb("hu3", [P, NT, HC], BF16)
        hur = sb("hur", [P, 2, NT, H])
        ew = sb("ew", [P, H, NT])
        nege = sb("nege", [P, H, NT])
        qa = sb("qa", [P, NT, HC])
        qd = sb("qd", [P, NT, HC])
        self_ = sb("self", [P, NT])
        qs = sb("qs", [P, NT, H])
        negm = sb("negm", [P, KT * H])
        den = sb("den", [P, KT * H])
        negmc = sb("negmc", [P, KT * H])
        nml = sb("nml", [P, KT * H])
        okc = sb("okc", [P, 2, NT])
        okm = sb("okm", [P, 4])
        flag = sb("flag", [1, 1], I32)
        unused = sb("unused", [1, 16])
        epsb = sb("epsb", [P, 1])
        tinyb = sb("tinyb", [P, 1])
        minus2 = sb("minus2", [P, 1])

        arena = sb("arena", [P, 18432])

        def part(start, *dims):
            size = int(np.prod(dims))
            view = arena[:, start:start + size]
            if len(dims) == 2:
                view = view.rearrange("p (a b) -> p a b", a=dims[0])
            if len(dims) == 3:
                view = view.rearrange("p (a b c) -> p a b c", a=dims[0], b=dims[1])
            return view

        mask = part(0, NT * N // 4).bitcast(F8).rearrange("p (a b) -> p a b", a=NT)
        rec = part(8192, 4, BLK)
        wgt = part(10240, 4, BLK)
        msg = part(12288, NT, D)
        mstage = part(15872, BLK).bitcast(F8).rearrange("p (a b) -> p a b", a=4)
        xs = part(14336, BLK)
        zr = part(14848, KT, D)
        zt = part(15360, BLK)
        stage = part(14336, 3 * P)
        graw = sc[:, 0, 0:4 * NG].rearrange("p (c g d) -> p c g d", c=4, g=3)

        neb = part(0, H, N)
        nmb = part(6144, H, BLK)
        tt = part(7680, 4, BLK)
        uu = part(9728, UU, BLK)
        att = part(12800, 2, BLK)
        nsb, esb, tr_, tz_, uv_, nn_, oe_ = (part(13824 + k * BLK, BLK) for k in range(7))
        osb = part(17408, KT, D)
        nsb_last = part(17920, BLK)
        work = [(tr_, tz_, uv_, nn_)] * 2
        work_last = [work[0], (tt[:, 0, :], tt[:, 1, :], tt[:, 2, :], tt[:, 3, :])]
        banks = [(5, 6, 7, 4)] * 2
        banks_last = [banks[0], (0, 1, 2, 3)]

        ps = ctx.enter_context(nc.psum_tensor("ps", [P, 8, 512], F32))

        x_in = [sem(f"x_in{g}") for g in range(NB)]
        weights_in = sem("weights_in")
        gru_w_in = sem("gru_w_in")
        diag_in = sem("diag_in")
        col_in = [sem(f"col_in{s}") for s in range(NB)]
        row_in = [sem(f"row_in{s}") for s in range(2)]
        stored = sem("stored")
        const_set = sem("const_set")
        wprep = sem("wprep")
        wcopied = sem("wcopied")
        p_stat = sem("p_stat")
        recip_ln0 = sem("recip_ln0")
        p_rstd = sem("p_rstd")
        p_z = sem("p_z")
        p_zt = sem("p_zt")
        p_ztc = sem("p_ztc")
        p_msg = sem("p_msg")
        p_msgc = sem("p_msgc")
        vp = sem("vp")
        adj_t = sem("adj_t")
        ln_adj = sem("ln_adj")
        recip = sem("recip")
        mask_done = sem("mask_done")
        mask_kept = sem("mask_kept")
        sq_done = sem("sq_done")
        sens = sem("sens")
        wgt_done = sem("wgt_done")
        summed = sem("summed")
        f_xs = sem("f_xs")
        f_xt = sem("f_xt")
        f_stat = sem("f_stat")
        f_ln = sem("f_ln")
        f_rstd = sem("f_rstd")
        f_z = sem("f_z")
        f_zt = sem("f_zt")
        f_ztc = sem("f_ztc")
        f_keep = sem("f_keep")
        f_hw = sem("f_hw")
        f_hwa = sem("f_hwa")
        f_hwv = sem("f_hwv")
        vf = sem("vf")
        hu_split = sem("hu_split")
        vt = sem("vt")
        q_done = sem("q_done")
        e_done = sem("e_done")
        e_row = sem("e_row")
        e_rowa = sem("e_rowa")
        e_rowv = sem("e_rowv")
        ok_min = sem("ok_min")
        ok_t = sem("ok_t")
        flag_set = sem("flag_set")
        clean = sem("clean")
        pen_raw = sem("pen_raw")
        pen_done = sem("pen_done")
        pen_own = sem("pen_own")
        max_done = sem("max_done")
        sc_done = sem("sc_done")
        den_done = sem("den_done")
        ln_done = sem("ln_done")
        nml_done = sem("nml_done")
        bc_done = sem("bc_done")
        nmb_done = sem("nmb_done")
        att_t = sem("att_t")
        att_done = sem("att_done")
        t_done = sem("t_done")
        u_done = sem("u_done")
        early_t = sem("early_t")
        early_a = sem("early_a")
        early_d = sem("early_d")
        early_mm = sem("early_mm")
        early_ns = sem("early_ns")
        ns_mm = sem("ns_mm")
        es_mm = sem("es_mm")
        sup_out = sem("sup_out")
        g_part = sem("g_part")
        g_act = sem("g_act")
        g_dve = sem("g_dve")
        vg = sem("vg")
        o_sum = sem("o_sum")
        o_t = sem("o_t")
        o_done = sem("o_done")

        adj_cols = adj.rearrange("(b k p) (q c) -> b q p k c", k=KT, p=P, q=NB)
        adj_rows = adj.rearrange("(t p) n -> t p n", p=P)
        out_blocks = out.rearrange("(b k p) d -> b p k d", k=KT, p=P)

        GATE = 6
        CELL = 3
        OWN = 2 * CELL

        general_step = sem("general_step")
        g_x_in = sem("g_x_in")
        g_row_in = sem("g_row_in")
        g_stored = sem("g_stored")
        a_row, w_row = row[:, 0, :], row[:, 1, :]
        pos, neg = sc[:, 0, :], sc[:, 1, :]
        none = col[:, 0, :, :].rearrange("p k c -> p (k c)")
        score = col[:, 1, :, :].rearrange("p k c -> p (k c)")
        score2 = col[:, 2, :, :].rearrange("p k c -> p (k c)")
        e_all = part(0, 2 * H, N)
        g_msg = part(12288, NT, D)
        quad = part(14336, BLK)
        cur, z = part(14848, D), part(14976, D)
        zt_g = part(15104, P)
        e_col = part(15232, 2 * H, NT)
        dg6 = part(15328, 2 * H, P)
        sup2 = part(16096, 2, P)
        sup_rows = part(16352, 2, D)
        g_r, g_z, g_n, g_d, g_sum, g_out = (part(16608 + k * P, P) for k in range(6))
        nbr = part(17376, 2 * H)
        g_small = part(17400, 8)
        G_MAX, G_BIAS, G_DEN, G_RDEN = range(4)

        def product_steps(tag):
            return [f"{tag} {what} {q}" for q in range(NB) for what in ("transpose", "copy", "multiply")]

        LN = ["stats", "aggregate", "ln", "rsqrt", "newton 0", "newton 1", "newton 2", "newton 3",
              "normalise", "relu", "transpose z", "copy z"]
        MESSAGES = ["fetch"] + LN + ["times w0", "add b0"]
        WEIGHTS = (["square", "clamp", "reciprocal", "r", "q", "exp", "below 1", "not 0"] + product_steps("sum")
                   + ["x1", "keep x1"] + LN + ["keep h2", "keep h2t", "times W", "keep hw"])
        SIGNS = ["no diagonal", "pos", "neg"]
        NEIGHBOURS = (SIGNS + product_steps("plus") + product_steps("minus")
                      + ["keep plus", "e_plus", "e_minus", "leaky plus", "leaky minus"])
        SPREAD = ["diagonals", "spread", "copy plus", "copy minus"]
        HEAD = ["plus score", "minus score", "both", "outside", "max", "bias", "exp", "denominator",
                "reciprocal", "probability"]
        CELLS = ["gates", "sigmoid r", "sigmoid z", "times r", "add in", "tanh", "h - n", "times z", "add n"]
        ATTEND = SIGNS + ["none"] + product_steps("node")
        for h in range(H):
            ATTEND += [f"{h} {name}" for name in HEAD] + product_steps(f"{h} edge")
        ATTEND += ["keep node", "keep edge", "transpose supports", "copy supports"]
        for c in range(2):
            ATTEND += [f"{c} {name}" for name in CELLS]
        ATTEND += ["add cells", "transpose out", "out"]
        S1 = 1
        S2 = S1 + len(MESSAGES) * NT
        S3 = S2 + len(WEIGHTS) * NT
        S4 = S3 + len(NEIGHBOURS) * NT
        S5 = S4 + len(SPREAD) * NT

        block = ctx.enter_context(nc.Block())

        @block.sync
        def _(sp):
            sp.sem_inc(stored, 16)
            for g in range(NB):
                sp.dma_start(xb[:, KT * g:KT * g + KT, :], x.rearrange("(g t p) d -> g p t d", g=NB, p=P)[g])\
                    .then_inc(x_in[g], 16)
            for q in range(NB):
                sp.dma_start(col[:, q, :, :], adj_cols[0, q]).then_inc(col_in[q], 16)
            with nc.sync.Fori(1, NB) as b:
                for q in range(NB):
                    sp.wait_ge(adj_t, NT * b - NT + KT * q + KT)
                    sp.dma_start(col[:, q, :, :], adj_cols[bass.ds(b, 1), q, :, :, :]
                                 .rearrange("o p k c -> (o p) k c")).then_inc(col_in[q], 16)
            for q in range(NB):
                sp.wait_ge(early_t, KT * q + KT)
                sp.dma_start(col[:, q, :, :], adj_cols[0, q]).then_inc(col_in[q], 16)
            def next_block(b, first):
                for q in range(NB):
                    if q == NB - 1 and not first:
                        store(b - 1)
                    sp.wait_ge(att_t, NT * b + KT * q + KT)
                    sp.dma_start(col[:, q, :, :], adj_cols[bass.ds(b + 1, 1), q, :, :, :]
                                 .rearrange("o p k c -> (o p) k c")).then_inc(col_in[q], 16)

            def store(f):
                sp.wait_ge(o_done, f + 1)
                sp.dma_start(out_blocks[bass.ds(f, 1), :, :, :].rearrange("o p k d -> (o p) k d"),
                             osb).then_inc(stored, 16)

            next_block(0, True)
            with nc.sync.Fori(1, NB - 1) as b:
                next_block(b, False)
            store(NB - 2)
            store(NB - 1)
            sp.wait_ge(stored, 16 * NB + 16)

            sp.wait_ge(flag_set, 1)
            signed = nc.sync.value_load(flag[0:1, 0:1], min_val=0, max_val=1)
            with nc.sync.If(signed != 0):
                sp.dma_start(xb[:, :, :], x.rearrange("(t p) d -> p t d", p=P)).then_inc(g_x_in, 16)
                sp.sem_inc(general_step, 1)
                sp.sem_inc(g_stored, 16)

                def load_rows(t, free):
                    sp.wait_ge(general_step, free)
                    sp.dma_start(row[:, 0:1, :], adj_rows[bass.ds(t, 1), :, :]
                                 .rearrange("o p n -> p o n")).then_inc(g_row_in, 16)

                for start, steps in ((S2, WEIGHTS), (S3, NEIGHBOURS)):
                    with nc.sync.Fori(0, NT) as t:
                        load_rows(t, len(steps) * t + start)
                with nc.sync.Fori(0, NT) as t:
                    sp.wait_ge(g_stored, 16 * t + 16)
                    load_rows(t, len(ATTEND) * t + S5)
                    sp.wait_ge(general_step, len(ATTEND) * t + S5 + len(ATTEND))
                    sp.dma_start(out[bass.ds(P * t, P), :], g_out).then_inc(g_stored, 16)
                sp.wait_ge(g_stored, 16 * NT + 16)

        @block.gpsimd
        def _(pool):
            pool.memset(ident[:, :], 0.0).then_inc(const_set, 1)
            pool.memset(ones[:, :], 1.0).then_inc(const_set, 1)
            pool.memset(epsb[:, :], EPS).then_inc(const_set, 1)
            pool.memset(tinyb[:, :], TINY).then_inc(const_set, 1)
            pool.memset(minus2[:, :], -2.0).then_inc(const_set, 1)
            pool.memset(hu3[:, :, :], 1.0).then_inc(const_set, 1)
            pool.wait_ge(const_set, 6)
            pool.affine_select(out=ident[:, :], in_=ident[:, :], compare_op=ALU.not_equal, fill=1.0,
                               base=0, pattern=[[-1, P]], channel_multiplier=1).then_inc(const_set, 1)
            pool.wait_ge(const_set, 7)
            pool.tensor_scalar(offdiag[:, :], ident[:, :], -1.0, 1.0, ALU.mult, ALU.add).then_inc(const_set, 1)

            pool.tensor_scalar(outdiag[:, :], ident[:, :], OUT, 0.0, ALU.mult, ALU.add).then_inc(const_set, 1)

            pool.wait_ge(x_in[NB - 1], 16)
            pool.dma_start(de[:, :], bass.AP(adj.tensor, 0, [[N + 1, P], [P * (N + 1), NT], [1, 1]])
                           .rearrange("p t o -> p (t o)"), allow_slow_non_contiguous=True).then_inc(diag_in, 16)
            for c, b_ in enumerate((e_bih, e_bhh, n_bih, n_bhh)):
                pool.dma_start(bi[:, c, :], b_.rearrange("(g p) -> p g", p=P),
                               allow_slow_non_contiguous=True).then_inc(diag_in, 16)

            for c, w in enumerate((e_wih, e_whh, n_wih, n_whh)):
                pool.dma_start(graw[:, c, :, :], w.rearrange("(g p) d -> p g d", p=P)).then_inc(gru_w_in, 16)
            pool.sem_inc(f_keep, 2)
            for t in range(2):
                pool.dma_start(row[:, t, :], adj_rows[t]).then_inc(row_in[t], 16)

            def keep_h2(f):
                pool.wait_ge(f_z, f + 1)
                pool.tensor_copy(h2[:, bass.ts(f, KT), :], zr).then_inc(f_keep, 1)

            def keep_h2t(f):
                pool.wait_ge(f_ztc, f + 1)
                pool.tensor_copy(h2t[:, bass.ts(f, BLK)], zt).then_inc(f_keep, 1)

            def pen_quarter(t, q):
                cols = slice(q * BLK, (q + 1) * BLK)
                pool.wait_ge(row_in[t % 2], 16 * (t // 2 + 1))
                pool.tensor_scalar(pen[:, t % 2, cols], row[:, t % 2, cols], 0.0, OUT,
                                   ALU.is_le, ALU.mult).then_inc(pen_raw, 1)

            def pen_diagonal(t):
                spot = pen[:, t % 2, P * t:P * t + P]
                pool.affine_select(out=spot, in_=spot, compare_op=ALU.not_equal, fill=OUT, base=0,
                                   pattern=[[-1, P]], channel_multiplier=1).then_inc(pen_done, 1)

            def layer0(b, first):
                for j in range(NT):
                    pool.wait_ge(mask_done, NT * b + j + 1)
                    pool.tensor_copy(mask[:, j, bass.ts(b, BLK)].bitcast(I32), mstage[:, j % 4, :].bitcast(I32))\
                        .then_inc(mask_kept, 1)
                    if first and j % 2:
                        pen_quarter(j // 2 // NB, j // 2 % NB)
                    if not first and j == 8:
                        keep_h2(b - 1)
                    if not first and j == 10:
                        keep_h2t(b - 1)

            layer0(0, True)
            pool.wait_ge(pen_raw, 2 * NB)
            for t in range(2):
                pen_diagonal(t)
                pool.dma_start(row[:, t, :], adj_rows[t + 2]).then_inc(row_in[t], 16)
            with nc.gpsimd.Fori(1, NB) as b:
                layer0(b, False)
            keep_h2(NB - 1)
            keep_h2t(NB - 1)

            def pen_of(t):
                pool.wait_ge(row_in[t % 2], 16 * (t // 2 + 1))
                pool.wait_ge(sc_done, H * (t - 1))
                pool.tensor_scalar(pen[:, t % 2, :], row[:, t % 2, :], 0.0, OUT,
                                   ALU.is_le, ALU.mult).then_inc(pen_raw, 1)
                pool.wait_ge(pen_raw, 3 * NB + t - KT)
                pen_diagonal(t)
                if t + 2 < NT:
                    pool.dma_start(row[:, t % 2, :], adj_rows[t + 2]).then_inc(row_in[t % 2], 16)

            def clean_of(b, q):
                pool.wait_ge(col_in[q], 16 * (NB + b + 1))
                if q == b:
                    spot = col[:, q, :, :]
                    pool.affine_select(out=spot, in_=spot, compare_op=ALU.not_equal, fill=0.0, base=0,
                                       pattern=[[-P, KT], [1, BLK]], channel_multiplier=-1).then_inc(clean, 1)
                else:
                    pool.sem_inc(clean, 1)

            for t in range(2):
                pool.wait_ge(pen_own, t + 1)
                pool.dma_start(row[:, t, :], adj_rows[t + 4]).then_inc(row_in[t], 16)
            clean_of(0, 0)
            for k in range(KT):
                pool.wait_ge(early_a, NT - KT + k + 1)
                spot = att[:, k % 2, k * P:(k + 1) * P]
                pool.affine_select(out=spot, in_=spot, compare_op=ALU.not_equal, fill=0.0, base=0,
                                   pattern=[[-1, P]], channel_multiplier=1).then_inc(early_d, 1)
                pool.wait_ge(sc_done, H * (KT - 1))
                pen_quarter(KT, k)
            pool.wait_ge(pen_raw, 3 * NB)
            pen_diagonal(KT)
            pool.dma_start(row[:, 0, :], adj_rows[KT + 2]).then_inc(row_in[0], 16)
            for b in range(NB):
                for q in range(NB):
                    if b or q:
                        clean_of(b, q)
                    if b + 1 < NB and (b or q):
                        pen_of(KT * (b + 1) + q)

        @block.tensor
        def _(pe):
            mm, transpose = nc.tensor.matmul, nc.tensor.transpose

            def transpose_z(g):
                pe.wait_ge(p_z, g + 1)
                if g >= 2:
                    pe.wait_ge(p_ztc, g - 1)
                for k in range(KT):
                    last = transpose(ps[:, 5 + g % 2, k * P:(k + 1) * P], h2[:, KT * g + k, :], ident[:, :])
                last.then_inc(p_zt, 1)

            pe.wait_ge(const_set, 9)
            transpose_z(0)
            pe.wait_ge(weights_in, 64)
            for g in range(NB):
                if g + 1 < NB:
                    transpose_z(g + 1)
                pe.wait_ge(p_ztc, g + 1)
                if g >= 2:
                    pe.wait_ge(p_msgc, g - 1)
                for k in range(KT):
                    t = KT * g + k
                    last = mm(ps[:, (4, 7)[g % 2], k * D:(k + 1) * D], h2t[:, t * P:(t + 1) * P], w0s[:, :],
                              start=True, stop=True)
                last.then_inc(p_msg, 1)

            def transpose_w():
                for h in range(H):
                    last = transpose(ps[:, 7, h * D:(h + 1) * D], wcat[:, h * D:(h + 1) * D], ident[:, :])
                last.then_inc(wprep, 1)

            def w_times_a():
                pe.wait_ge(wcopied, 1)
                for h in range(H):
                    last = mm(ps[:, 6, 2 * h:2 * h + 2], stage[:, h * D:(h + 1) * D], gas[:, h, :],
                              start=True, stop=True)
                last.then_inc(wprep, 1)

            def adj_chunk(b, j):
                q = j // KT
                if j % KT == 0:
                    pe.wait_ge(col_in[q], 16 * b + 16)
                if not (isinstance(b, int) and b == 0 and j < 4):
                    pe.wait_ge(wgt_done, NT * b + j - 3)
                for k in range(KT):
                    last = transpose(ps[:, j % 4, k * P:(k + 1) * P],
                                     col[:, q, k, (j % KT) * P:(j % KT + 1) * P], ident[:, :])
                last.then_inc(adj_t, 1)

            def sum_chunk(b, j):
                pe.wait_ge(wgt_done, NT * b + j + 1)
                mm(ps[:, 4, :], msg[:, j, :], wgt[:, j % 4, :], start=(j == 0), stop=(j == NT - 1))\
                    .then_inc(summed, 1)

            def hw_chunk(f, k):
                mm(ps[:, (7, 5, 7, 6)[k], 0:HWC], zt[:, k * P:(k + 1) * P], wcat[:, :],
                   start=True, stop=True).then_inc(f_hw, 1)

            def finish(f, step):
                if step == 3:
                    pe.wait_ge(f_xs, f + 1)
                    for k in range(KT):
                        last = transpose(ps[:, 5, k * P:(k + 1) * P], xs[:, k * P:(k + 1) * P], ident[:, :])
                    last.then_inc(f_xt, 1)
                if step == 8:
                    pe.wait_ge(f_z, f + 1)
                    for k in range(KT):
                        last = transpose(ps[:, 6, k * P:(k + 1) * P], zr[:, k, :], ident[:, :])
                    last.then_inc(f_zt, 1)
                if step == 9:
                    pe.wait_ge(f_ztc, f + 1)
                    hw_chunk(f, 0)
                    hw_chunk(f, 1)
                if step == 11:
                    pe.wait_ge(f_hwa, 2 * f + 1)
                    hw_chunk(f, 2)
                    hw_chunk(f, 3)

            def layer0(b, first):
                for j in range(NT):
                    adj_chunk(b, j)
                    if not first:
                        finish(b - 1, j)
                    if j >= 3:
                        sum_chunk(b, j - 3)
                    elif not first:
                        sum_chunk(b - 1, NT - 3 + j)
                    if first and j == 2:
                        pe.wait_ge(p_msgc, NB)
                    if first and j == 5:
                        transpose_w()
                    if first and j == 10:
                        w_times_a()

            layer0(0, True)
            with nc.tensor.Fori(1, NB) as b:
                layer0(b, False)
            for j in range(3):
                sum_chunk(NB - 1, NT - 3 + j)
            def neighbour_sums(bank, first, end):
                for t in range(NT):
                    for j in range(first, end):
                        last = mm(ps[:, bank, t * HC:(t + 1) * HC], mask[:, j, t * P:(t + 1) * P], hu3[:, j, :],
                                  start=(j == first), stop=(j == end - 1))
                last.then_inc(q_done, 1)

            for step in range(NT):
                finish(NB - 1, step)
                if step == 3:
                    pe.wait_ge(hu_split, 1)
                    pe.wait_ge(mask_kept, NT * NB)
                    neighbour_sums(4, 0, NT - KT)
                if step == 9:
                    pe.wait_ge(gru_w_in, 64)
                    for c in range(4):
                        for g in range(3):
                            last = transpose(ps[:, c, g * D:(g + 1) * D], graw[:, c, g, :], ident[:, :])
                        last.then_inc(wprep, 1)
            pe.wait_ge(hu_split, 2)
            neighbour_sums(5, NT - KT, NT)
            pe.wait_ge(e_done, 2)
            pe.wait_ge(wcopied, 6)
            for n in range(H * NB):
                if n >= 4:
                    pe.wait_ge(*((e_rowa, (n - 4) // 2 + 1) if n % 2 == 0 else (e_rowv, (n - 4) // 2 + 1)))
                for k in range(KT):
                    t = KT * (n % NB) + k
                    last = transpose(ps[:, 1 + n % 4, k * P:(k + 1) * P],
                                     nege[:, n // NB, t:t + 1].broadcast_to([P, P]), ident[:, :])
                last.then_inc(e_row, 1)
                if n == 5:
                    pe.wait_ge(ok_min, 1)
                    transpose(ps[0:1, 0, 256:256 + P], okm[:, 0:1], ident[:, :]).then_inc(ok_t, 1)
            def early_chunk(j):
                if j >= 2:
                    pe.wait_ge(early_a, j - 1)
                for k in range(KT):
                    last = transpose(ps[:, 5 + j % 2, k * P:(k + 1) * P],
                                     col[:, j // KT, k, (j % KT) * P:(j % KT + 1) * P], ident[:, :])
                last.then_inc(early_t, 1)

            pe.wait_ge(f_keep, 2 * NB + 2)
            early_chunk(0)
            for j in range(NT):
                if j + 1 < NT:
                    early_chunk(j + 1)
                pe.wait_ge(*((early_a, j + 1) if j < NT - KT else (early_d, j + 1 - (NT - KT))))
                mm(ps[:, 7, :], h2[:, j, :], att[:, j % 2, :], start=(j == 0), stop=(j == NT - 1))\
                    .then_inc(early_mm, 1)

            def att_chunk(b, j):
                q = j // KT
                if j % KT == 0:
                    pe.wait_ge(clean, NB * b + q + 1)
                if not (isinstance(b, int) and b == 0 and j < 2):
                    pe.wait_ge(att_done, NT * b + j - 1)
                for k in range(KT):
                    last = transpose(ps[:, j % 2, k * P:(k + 1) * P],
                                     col[:, q, k, (j % KT) * P:(j % KT + 1) * P], ident[:, :])
                last.then_inc(att_t, 1)

            def supports(b, j, first, last_):
                if j == 0 and not first:
                    pe.wait_ge(sup_out, 2 * b)
                pe.wait_ge(att_done, NT * b + j + 1)
                if not last_:
                    mm(ps[:, 2, :], h2[:, j, :], att[:, j % 2, :], start=(j == 0), stop=(j == NT - 1))\
                        .then_inc(ns_mm, 1)
                for h in range(H):
                    n = H * j + h
                    pe.wait_ge(u_done, H * NT * b + n + 1)
                    mm(ps[:, 3, :], hw[:, j, h * D:(h + 1) * D], uu[:, n % UU, :],
                       start=(n == 0), stop=(n == H * NT - 1)).then_inc(es_mm, 1)

            def broadcast(s):
                pe.wait_ge(nml_done, s + 1)
                for h in range(H):
                    for k in range(KT):
                        n = H * k + h
                        last = transpose(ps[:, 4 + h, k * P:(k + 1) * P],
                                         nml[:, n:n + 1].broadcast_to([P, P]), ident[:, :])
                    last.then_inc(bc_done, 1)

            def gate(f, c, g, bank, x_part=True, h_part=True):
                support = esb if c else nsb_last if isinstance(f, int) and f == NB - 1 else nsb
                if x_part:
                    mm(ps[:, bank, :], wt[:, 2 * c, g * D:(g + 1) * D], support,
                       start=True, stop=(g == 2)).then_inc(g_part, 1)
                if h_part:
                    mm(ps[:, bank, :], wt[:, 2 * c + 1, g * D:(g + 1) * D], h2t[:, bass.ts(f, BLK)],
                       start=(g == 2), stop=True).then_inc(g_part, 1)

            def out_transpose(f, rows):
                pe.wait_ge(o_sum, f + 1)
                for k in range(KT):
                    last = transpose(ps[:, 7, k * P:(k + 1) * P], rows[:, k * P:(k + 1) * P], ident[:, :])
                last.then_inc(o_t, 1)

            def gru_step(f, j):
                if 1 <= j <= 10:
                    c, part_ = (j - 1) // 5, (j - 1) % 5
                    g = part_ // 2
                    if part_ == 0:
                        pe.wait_ge(sup_out, 2 * f + c + 1)
                        if c == 1:
                            pe.wait_ge(g_act, 6 * f + 1)
                    if c == 1 and part_ == 2:
                        pe.wait_ge(g_act, 6 * f + 2)
                    if c == 1 and part_ == 4:
                        pe.wait_ge(g_dve, 4 * f + 2)
                    if part_ < 4:
                        gate(f, c, g, banks[c][g], part_ % 2 == 0, part_ % 2 == 1)
                    else:
                        gate(f, c, 2, banks[c][2], x_part=False)
                        gate(f, c, 2, banks[c][3], h_part=False)
                if j == 14:
                    out_transpose(f, uv_)

            def layer1(b, first, last_):
                for j in range(NT):
                    if j + 1 < NT:
                        att_chunk(b, j + 1)
                    elif not last_:
                        att_chunk(b + 1, 0)
                    if not last_ and j == 15:
                        broadcast(b + 1)
                    supports(b, j, first, last_)
                    if not first:
                        gru_step(b - 1, j)

            pe.wait_ge(e_rowv, H * NB // 2)
            pe.wait_ge(flag_set, 1)
            att_chunk(0, 0)
            broadcast(0)
            layer1(0, True, False)
            with nc.tensor.Fori(1, NB - 1) as b:
                layer1(b, False, False)
            layer1(NB - 1, False, True)
            pe.wait_ge(o_done, NB - 1)
            pe.wait_ge(early_ns, 1)
            for c in range(2):
                if c:
                    pe.wait_ge(sup_out, 2 * NB - 1)
                for g in range(2):
                    gate(NB - 1, c, g, banks_last[c][g])
                gate(NB - 1, c, 2, banks_last[c][2], x_part=False)
                gate(NB - 1, c, 2, banks_last[c][3], h_part=False)
            out_transpose(NB - 1, oe_)

            def turn(at, steps, name):
                pe.wait_ge(general_step, at + steps.index(name))

            def product(at, steps, tag, rows, bank, moving, first=True, last=True):
                for q in range(NB):
                    turn(at, steps, f"{tag} transpose {q}")
                    for k in range(KT):
                        done = transpose(ps[:, 0, k * P:(k + 1) * P],
                                         rows[:, (KT * q + k) * P:(KT * q + k + 1) * P], ident[:, :])
                    done.then_inc(general_step, 1)
                    turn(at, steps, f"{tag} multiply {q}")
                    for k in range(KT):
                        j = KT * q + k
                        done = mm(bank, quad[:, k * P:(k + 1) * P], moving(j),
                                  start=(first and j == 0), stop=(last and j == NT - 1))
                    done.then_inc(general_step, 1)

            def transpose_z(at, steps):
                turn(at, steps, "transpose z")
                transpose(ps[:, 0, 0:P], z, ident[:, :]).then_inc(general_step, 1)

            pe.wait_ge(flag_set, 1)
            signed = nc.tensor.value_load(flag[0:1, 0:1], min_val=0, max_val=1)
            with nc.tensor.If(signed != 0):
                with nc.tensor.Fori(0, NT) as t:
                    at = len(MESSAGES) * t + S1
                    transpose_z(at, MESSAGES)
                    turn(at, MESSAGES, "times w0")
                    mm(ps[:, 1, 0:D], zt_g, w0s[:, :], start=True, stop=True).then_inc(general_step, 1)
                with nc.tensor.Fori(0, NT) as t:
                    at = len(WEIGHTS) * t + S2
                    product(at, WEIGHTS, "sum", w_row, ps[:, 1, 0:D], lambda j: g_msg[:, j, :])
                    transpose_z(at, WEIGHTS)
                    turn(at, WEIGHTS, "times W")
                    mm(ps[:, 1, 0:HWC], zt_g, wcat[:, :], start=True, stop=True).then_inc(general_step, 1)
                with nc.tensor.Fori(0, NT) as t:
                    at = len(NEIGHBOURS) * t + S3
                    product(at, NEIGHBOURS, "plus", pos, ps[:, 1, 0:2 * H], lambda j: hw[:, j, H * D:HWC])
                    product(at, NEIGHBOURS, "minus", neg, ps[:, 2, 0:2 * H], lambda j: hw[:, j, H * D:HWC])
                with nc.tensor.Fori(0, NT) as t:
                    turn(len(SPREAD) * t + S4, SPREAD, "spread")
                    for s in range(2):
                        done = mm(ps[:, 1 + s, 0:H * P], ones[:, :], dg6[:, H * s:H * s + H, :]
                                  .rearrange("p h c -> p (h c)"), start=True, stop=True)
                    done.then_inc(general_step, 1)
                with nc.tensor.Fori(0, NT) as t:
                    at = len(ATTEND) * t + S5
                    product(at, ATTEND, "node", a_row, ps[:, 1, 0:D], lambda j: h2[:, j, :])
                    for h in range(H):
                        product(at, ATTEND, f"{h} edge", w_row, ps[:, 2, 0:D],
                                lambda j: hw[:, j, h * D:(h + 1) * D], first=(h == 0), last=(h == H - 1))
                    turn(at, ATTEND, "transpose supports")
                    for s in range(2):
                        done = transpose(ps[:, 0, s * P:(s + 1) * P], sup_rows[:, s, :], ident[:, :])
                    done.then_inc(general_step, 1)
                    hs = h2t[:, bass.ts(t, P)]
                    for c in range(2):
                        turn(at, ATTEND, f"{c} gates")
                        for g in range(2):
                            mm(ps[:, 3 + g, 0:P], wt[:, 2 * c, g * D:(g + 1) * D], sup2[:, c, :],
                               start=True, stop=False)
                            mm(ps[:, 3 + g, 0:P], wt[:, 2 * c + 1, g * D:(g + 1) * D], hs,
                               start=False, stop=True)
                        mm(ps[:, 5, 0:P], wt[:, 2 * c + 1, 2 * D:3 * D], hs, start=True, stop=True)
                        mm(ps[:, 6, 0:P], wt[:, 2 * c, 2 * D:3 * D], sup2[:, c, :], start=True, stop=True)\
                            .then_inc(general_step, 1)
                    turn(at, ATTEND, "transpose out")
                    transpose(ps[:, 0, 0:P], g_sum, ident[:, :]).then_inc(general_step, 1)

        @block.scalar
        def _(act):
            activation = nc.scalar.activation

            act.dma_start(w0s[:, :], w0).then_inc(weights_in, 16)
            act.dma_start(b0s[:, :], b0.rearrange("(o d) -> o d", o=1).broadcast_to([P, D])).then_inc(weights_in, 16)
            act.dma_start(wcat[:, 0:H * D].rearrange("p (h d) -> p h d", h=H),
                           gat_w.rearrange("h p d -> p h d")).then_inc(weights_in, 16)
            act.dma_start(gas[:, :, :], gat_a.rearrange("h (s p) o -> p h (s o)", s=2),
                           allow_slow_non_contiguous=True).then_inc(weights_in, 16)

            act.preload_act_table_set("natural_log_exp_and_others")
            act.wait_ge(const_set, 9)
            act.wait_ge(p_stat, 1)
            activation(rstd[:, :], mv[:, :, 1], ACT.Ln, bias=epsb[:, :]).then_inc(recip_ln0, 1)
            act.wait_ge(recip_ln0, 1)
            activation(rstd[:, :], rstd[:, :], ACT.Exp, scale=-0.5).then_inc(p_rstd, 1)
            for g in range(NB):
                act.wait_ge(p_zt, g + 1)
                activation(h2t[:, g * BLK:(g + 1) * BLK], ps[:, 5 + g % 2, :], ACT.Copy).then_inc(p_ztc, 1)

            def reciprocal(b, j):
                u = NT * b + j
                act.wait_ge(adj_t, u + 1)
                if not (isinstance(b, int) and b == 0 and j < 4):
                    act.wait_ge(sq_done, u - 3)
                activation(rec[:, j % 4, :], ps[:, j % 4, :], ACT.Ln, bias=tinyb[:, :]).then_inc(ln_adj, 1)
                act.wait_ge(ln_adj, u + 1)
                activation(rec[:, j % 4, :], rec[:, j % 4, :], ACT.Exp, scale=-1.0).then_inc(recip, 1)

            def sensitivity(b, j):
                act.wait_ge(sq_done, NT * b + j + 1)
                activation(wgt[:, j % 4, :], wgt[:, j % 4, :], ACT.Exp, bias=minus2[:, :], scale=-2.0)\
                    .then_inc(sens, 1)

            def finish(f, step):
                if step == 3:
                    act.wait_ge(summed, NT * f + NT)
                    activation(xs, ps[:, 4, :], ACT.Copy).then_inc(f_xs, 1)
                if step == 5:
                    act.wait_ge(f_stat, f + 1)
                    activation(rstd[:, 0:KT], mv[:, 0:KT, 1], ACT.Ln, bias=epsb[:, :]).then_inc(f_ln, 1)
                    act.wait_ge(f_ln, f + 1)
                    activation(rstd[:, 0:KT], rstd[:, 0:KT], ACT.Exp, scale=-0.5).then_inc(f_rstd, 1)
                if step == 8:
                    act.wait_ge(f_zt, f + 1)
                    act.wait_ge(f_keep, 2 * f + 2)
                    activation(zt, ps[:, 6, :], ACT.Copy).then_inc(f_ztc, 1)
                if step in (10, 12):
                    k = step - 10
                    act.wait_ge(f_hw, KT * f + k + 1)
                    activation(hw[:, bass.ds(KT * f + k, 1), :], ps[:, 7:8, 0:HWC], ACT.Copy).then_inc(f_hwa, 1)

            def layer0(b, first):
                for j in range(NT):
                    if not first:
                        finish(b - 1, j)
                    reciprocal(b, j)
                    if j:
                        sensitivity(b, j - 1)
                    elif not first:
                        sensitivity(b - 1, NT - 1)
                    if first and j == 7:
                        act.wait_ge(wprep, 1)
                        activation(stage, ps[:, 7, 0:H * D], ACT.Copy).then_inc(wcopied, 1)
                    if first and j == 12:
                        act.wait_ge(wprep, 2)
                        activation(wcat[:, H * D:HWC], ps[:, 6, 0:2 * H], ACT.Copy).then_inc(wcopied, 1)

            layer0(0, True)
            with nc.scalar.Fori(1, NB) as b:
                layer0(b, False)
            sensitivity(NB - 1, NT - 1)
            for step in range(NT):
                finish(NB - 1, step)
                if step == 12:
                    for c in range(4):
                        act.wait_ge(wprep, 3 + c)
                        activation(wt[:, c, :], ps[:, c, 0:NG], ACT.Copy).then_inc(wcopied, 1)

            def copy_row(n):
                act.wait_ge(e_row, n + 1)
                activation(neb[:, n // NB, (n % NB) * BLK:(n % NB + 1) * BLK], ps[:, 1 + n % 4, :],
                           ACT.Copy).then_inc(e_rowa, 1)

            def denominator(s, n):
                act.wait_ge(max_done, KT * H * s + n + 1)
                view = sc[:, n % 2, :]
                activation(view, view, ACT.Sigmoid, bias=negmc[:, n:n + 1], scale=-1.0,
                           accum_out=den[:, n:n + 1]).then_inc(den_done, 1)

            def logarithms(s):
                act.wait_ge(den_done, KT * H * s + KT * H)
                activation(den[:, :], den[:, :], ACT.Ln, scale=H * math.exp(2 * C)).then_inc(ln_done, 1)
                act.preload_act_table_set("sigmoid_and_others")

            def copy_nml(s):
                for h in range(H):
                    act.wait_ge(bc_done, H * s + h + 1)
                    if h == 0 and not (isinstance(s, int) and s == 0):
                        act.wait_ge(t_done, H * NT * s)
                    activation(nmb[:, h, :], ps[:, 4 + h, :], ACT.Copy).then_inc(nmb_done, 1)

            def copy_att(b, j):
                u = NT * b + j
                act.wait_ge(att_t, u + 1)
                if not (isinstance(b, int) and b == 0 and j < 2):
                    act.wait_ge(u_done, H * u - H)
                    if not (isinstance(b, int) and b == NB - 1 and j >= 2):
                        act.wait_ge(ns_mm, u - 1)
                if isinstance(b, int) and b == 0 and j < 2:
                    act.wait_ge(early_mm, NT)
                activation(att[:, j % 2, :], ps[:, j % 2, :], ACT.Copy).then_inc(att_done, 1)
                if isinstance(b, int) and b == 0 and j == 1:
                    activation(nsb_last, ps[:, 7, :], ACT.Copy).then_inc(early_ns, 1)

            def attention(b, j):
                for h in range(H):
                    n = H * j + h
                    if j == 0:
                        act.wait_ge(nmb_done, H * b + h + 1)
                    if not (isinstance(b, int) and b == 0 and n < 4):
                        act.wait_ge(u_done, H * NT * b + n - 3)
                    activation(tt[:, n % 4, :], nmb[:, h, :], ACT.Sigmoid, bias=ew[:, h, j:j + 1])\
                        .then_inc(t_done, 1)

            def supports_out(f):
                act.wait_ge(ns_mm, NT * f + NT)
                activation(nsb, ps[:, 2, :], ACT.Copy).then_inc(sup_out, 1)
                act.wait_ge(es_mm, H * NT * f + H * NT)
                activation(esb, ps[:, 3, :], ACT.Copy, scale=math.exp(C)).then_inc(sup_out, 1)

            def sigmoid(f, c, g, bufs, bank):
                act.wait_ge(g_part, 2 * GATE * f + GATE * c + 2 * g + 2)
                activation(bufs[g], ps[:, bank, :], ACT.Sigmoid, bias=gb[:, c, g:g + 1]).then_inc(g_act, 1)

            def tanh(f, c, bufs):
                act.wait_ge(g_dve, 4 * f + 2 * c + 2)
                activation(bufs[3], bufs[2], ACT.Tanh, bias=bi[:, 2 * c, 2:3]).then_inc(g_act, 1)

            def gru_step(f, j):
                if j == 1:
                    supports_out(f)
                if j in (4, 9):
                    if j == 9:
                        act.wait_ge(g_dve, 4 * f + 1)
                    sigmoid(f, j // 9, 0, work[0], banks[0][0])
                if j in (6, 11):
                    if j == 11:
                        act.wait_ge(vg, OWN * f + CELL)
                    sigmoid(f, j // 11, 1, work[0], banks[0][1])
                if j in (8, 13):
                    tanh(f, j // 13, work[0])

            def layer1(b, first, last_):
                for j in range(NT):
                    if not first:
                        gru_step(b - 1, j)
                    copy_att(b, j)
                    attention(b, j)
                    if not last_ and 0 < j <= KT * H:
                        denominator(b + 1, j - 1)
                    if not last_ and j == 14:
                        logarithms(b + 1)
                if not last_:
                    copy_nml(b + 1)

            def copy_early(j):
                act.wait_ge(early_t, j + 1)
                if j >= 2:
                    act.wait_ge(early_mm, j - 1)
                activation(att[:, j % 2, :], ps[:, 5 + j % 2, :], ACT.Copy).then_inc(early_a, 1)

            act.preload_act_table_set("sigmoid_and_others")
            early = 0
            for n in range(KT * H):
                if n < H:
                    copy_row(NB * n)
                    copy_row(NB * n + 2)
                if n:
                    for _ in range(2 if n <= 5 else 1):
                        copy_early(early)
                        early += 1
                    denominator(0, n - 1)
            denominator(0, KT * H - 1)
            logarithms(0)
            copy_nml(0)
            layer1(0, True, False)
            with nc.scalar.Fori(1, NB - 1) as b:
                layer1(b, False, False)
            layer1(NB - 1, False, True)
            act.wait_ge(es_mm, H * NT * NB)
            activation(esb, ps[:, 3, :], ACT.Copy, scale=math.exp(C)).then_inc(sup_out, 1)
            for c in range(2):
                if c:
                    act.wait_ge(u_done, H * NT * NB)
                for g in range(2):
                    sigmoid(NB - 1, c, g, work_last[c], banks_last[c][g])
                tanh(NB - 1, c, work_last[c])

            def general(at, steps, name, *args, **kwargs):
                act.wait_ge(general_step, at + steps.index(name))
                activation(*args, **kwargs).then_inc(general_step, 1)

            def inverse_deviation(at, steps):
                general(at, steps, "ln", rstd[:, 0:1], mv[:, 0, 1:2], ACT.Ln, bias=epsb[:, :])
                general(at, steps, "rsqrt", rstd[:, 0:1], rstd[:, 0:1], ACT.Exp, scale=-0.5)

            act.wait_ge(flag_set, 1)
            signed = nc.scalar.value_load(flag[0:1, 0:1], min_val=0, max_val=1)
            with nc.scalar.If(signed != 0):
                with nc.scalar.Fori(0, NT) as t:
                    inverse_deviation(len(MESSAGES) * t + S1, MESSAGES)
                with nc.scalar.Fori(0, NT) as t:
                    at = len(WEIGHTS) * t + S2
                    general(at, WEIGHTS, "exp", w_row, w_row, ACT.Exp, bias=minus2[:, :], scale=-2.0)
                    inverse_deviation(at, WEIGHTS)
                with nc.scalar.Fori(0, NT) as t:
                    at = len(ATTEND) * t + S5
                    for h in range(H):
                        general(at, ATTEND, f"{h} exp", score, score, ACT.Sigmoid,
                                bias=g_small[:, G_BIAS:G_BIAS + 1])
                    for c in range(2):
                        general(at, ATTEND, f"{c} sigmoid r", g_r, ps[:, 3, 0:P], ACT.Sigmoid,
                                bias=gb[:, c, 0:1])
                        general(at, ATTEND, f"{c} sigmoid z", g_z, ps[:, 4, 0:P], ACT.Sigmoid,
                                bias=gb[:, c, 1:2])
                        general(at, ATTEND, f"{c} tanh", g_n, g_r, ACT.Tanh, bias=bi[:, 2 * c, 2:3])

        @block.vector
        def _(dve):
            v = nc.vector

            held = [0]

            def hold(b):
                if not isinstance(b, int):
                    held[0] = (held[0] + 1) % 16
                    v.memset(unused[:, held[0]:held[0] + 1], 0.0)

            def chain(semaphore, count):
                made = [count]

                def step(ins):
                    made[0] = made[0] + 1
                    ins.then_inc(semaphore, 1)
                    dve.wait_ge(semaphore, made[0])
                return step

            def refine(step, r, m):
                w_ = nwt[:, 0:r.shape[1]]
                step(v.scalar_tensor_tensor(w_, m, EPS, r, ALU.add, ALU.mult))
                step(v.tensor_tensor(w_, w_, r, ALU.mult))
                step(v.tensor_scalar(w_, w_, -0.5, 1.5, ALU.mult, ALU.add))
                step(v.tensor_tensor(r, r, w_, ALU.mult))

            def add_bias(g):
                dve.wait_ge(p_msg, g + 1)
                v.tensor_tensor(msg[:, KT * g:KT * g + KT, :],
                                ps[:, (4, 7)[g % 2], :].rearrange("p (k d) -> p k d", k=KT),
                                b0s[:, :].rearrange("p (o d) -> p o d", o=1).broadcast_to([P, KT, D]),
                                ALU.add).then_inc(p_msgc, 1)

            for t in range(NT):
                if t % KT == 0:
                    dve.wait_ge(x_in[t // KT], 16)
                last = v.bn_stats(stat[:, t, :], xb[:, t, :])
            pro = chain(vp, 0)
            pro(last)
            for t in range(NT):
                last = v.bn_aggr(mv[:, t, :], stat[:, t, :])
            last.then_inc(p_stat, 1)
            dve.wait_ge(p_rstd, 1)
            refine(pro, rstd[:, :], mv[:, :, 1])
            for g in range(NB):
                for k in range(KT):
                    t = KT * g + k
                    last = v.tensor_scalar(h2[:, t, :], xb[:, t, :], mv[:, t, 0:1], rstd[:, t:t + 1],
                                           ALU.subtract, ALU.mult)
                pro(last)
                z_ = h2[:, KT * g:KT * g + KT, :]
                v.tensor_scalar(z_, z_, 0.0, None, ALU.max).then_inc(p_z, 1)
            for g in range(NB - 2):
                add_bias(g)
            add_bias(NB - 2)
            add_bias(NB - 1)
            dve.wait_ge(diag_in, 80)
            for c in range(2):
                pro(v.tensor_tensor(gb[:, c, :], bi[:, 2 * c, 0:2], bi[:, 2 * c + 1, 0:2], ALU.add))

            def squared(b, j):
                u = NT * b + j
                dve.wait_ge(recip, u + 1)
                if not (isinstance(b, int) and b == 0 and j < 4):
                    dve.wait_ge(mask_kept, u - 3)
                hold(b)
                v.tensor_scalar(mstage[:, j % 4, :], ps[:, j % 4, :], HUGE, 1.0, ALU.mult, ALU.min,
                                saturate=False).then_inc(mask_done, 1)
                if not (isinstance(b, int) and b == 0 and j < 4):
                    dve.wait_ge(summed, u - 3)
                r = rec[:, j % 4, :]
                v.scalar_tensor_tensor(wgt[:, j % 4, :], r, -2.0, r, ALU.add, ALU.mult).then_inc(sq_done, 1)

            def weigh(b, j):
                dve.wait_ge(sens, NT * b + j + 1)
                w_ = wgt[:, j % 4, :]
                v.scalar_tensor_tensor(w_, ps[:, j % 4, :], 1.0, w_, ALU.is_lt, ALU.mult).then_inc(wgt_done, 1)

            FIN = 8

            def finish(f, step):
                if step == 4:
                    dve.wait_ge(f_xt, f + 1)
                    fin = chain(vf, FIN * f)
                    dve.wait_ge(f_keep, 2 * f + 1)
                    rows = xb[:, bass.ts(f, KT), :]
                    fin(v.tensor_tensor(zr, ps[:, 5, :].rearrange("p (k d) -> p k d", k=KT), rows, ALU.add))
                    hold(f)
                    for k in range(KT):
                        last = v.bn_stats(stat[:, k, :], zr[:, k, :])
                    fin(last)
                    hold(f)
                    for k in range(KT):
                        last = v.bn_aggr(mv[:, k, :], stat[:, k, :])
                    last.then_inc(f_stat, 1)
                    fin(v.tensor_copy(rows, zr))
                if step == 6:
                    dve.wait_ge(f_rstd, f + 1)
                    fin = chain(vf, FIN * f + 3)
                    refine(fin, rstd[:, 0:KT], mv[:, 0:KT, 1])
                    for k in range(KT):
                        last = v.tensor_scalar(zr[:, k, :], zr[:, k, :], mv[:, k, 0:1],
                                               rstd[:, k:k + 1], ALU.subtract, ALU.mult)
                    fin(last)
                    v.tensor_scalar(zr, zr, 0.0, None, ALU.max).then_inc(f_z, 1)
                if step in (10, 12):
                    k = step - 9
                    dve.wait_ge(f_hw, KT * f + k + 1)
                    v.tensor_copy(hw[:, bass.ds(KT * f + k, 1), :], ps[:, (7, 5, 7, 6)[k]:(7, 5, 7, 6)[k] + 1, 0:HWC])\
                        .then_inc(f_hwv, 1)

            def layer0(b, first):
                for j in range(NT):
                    if j >= 1:
                        squared(b, j - 1)
                    elif not first:
                        squared(b - 1, NT - 1)
                    if j >= 2:
                        weigh(b, j - 2)
                    elif not first:
                        weigh(b - 1, NT - 2 + j)
                    if not first:
                        finish(b - 1, j)

            layer0(0, True)
            with nc.vector.Fori(1, NB) as b:
                layer0(b, False)
            squared(NB - 1, NT - 1)
            weigh(NB - 1, NT - 2)
            weigh(NB - 1, NT - 1)

            tr = chain(vt, 0)
            hu = hw[:, :, H * D:H * D + 2 * H].rearrange("p t (h s) -> p t h s", s=2)[:, :, :, 0]

            def split_scores(first, end):
                dve.wait_ge(f_hwa, end // 2)
                dve.wait_ge(f_hwv, end // 2)
                u, parts = hu[:, first:end], hu3[:, first:end, :]
                rest, rest2 = hur[:, 0, first:end], hur[:, 1, first:end]
                tr(v.tensor_copy(parts[:, :, 0:H], u))
                tr(v.tensor_tensor(rest, u, parts[:, :, 0:H], ALU.subtract))
                tr(v.tensor_copy(parts[:, :, H:2 * H], rest))
                tr(v.tensor_tensor(rest2, rest, parts[:, :, H:2 * H], ALU.subtract))
                v.tensor_copy(parts[:, :, 2 * H:3 * H], rest2).then_inc(hu_split, 1)

            split_scores(0, NT - KT)
            for step in range(NT):
                finish(NB - 1, step)
            split_scores(NT - KT, NT)

            tr(v.tensor_scalar(self_[:, :], de[:, :], 0.0, None, ALU.is_gt))
            dve.wait_ge(hu_split, 2)
            tr(v.tensor_tensor(qd[:, :, :], hu3[:, :, :], self_[:, :].rearrange("p (t o) -> p t o", o=1)
                               .broadcast_to([P, NT, HC]), ALU.mult))
            banks_q = [ps[:, b, 0:NT * HC].rearrange("p (t c) -> p t c", t=NT) for b in (4, 5)]
            dve.wait_ge(q_done, 1)
            tr(v.tensor_tensor(qa[:, :, :], banks_q[0], qd[:, :, :], ALU.subtract))
            dve.wait_ge(q_done, 2)
            tr(v.tensor_tensor(qa[:, :, :], qa[:, :, :], banks_q[1], ALU.add))
            sums = qa[:, :, :]
            tr(v.tensor_reduce(qs[:, :, :], sums[:, :, 0:3 * H].rearrange("p t (s h) -> p t h s", s=3),
                               AX.X, ALU.add))
            v.scalar_tensor_tensor(ew[:, :, :], qs[:, :, :].rearrange("p t h -> p h t"), 0.2,
                                   qs[:, :, :].rearrange("p t h -> p h t"), ALU.mult, ALU.max).then_inc(e_done, 1)
            dve.wait_ge(e_done, 1)
            v.tensor_scalar(nege[:, :, :], ew[:, :, :], -1.0, None, ALU.mult).then_inc(e_done, 1)
            v.tensor_scalar(okc[:, 0, :], sums[:, :, 3 * H], 0.0, None, ALU.is_ge)
            tr(v.tensor_scalar(okc[:, 1, :], de[:, :], 0.0, None, ALU.is_ge))
            v.tensor_reduce(okm[:, 0:1], okc[:, :, :], AX.XY, ALU.min).then_inc(ok_min, 1)

            def copy_row(n):
                dve.wait_ge(e_row, n + 1)
                v.tensor_copy(neb[:, n // NB, (n % NB) * BLK:(n % NB + 1) * BLK], ps[:, 1 + n % 4, :])\
                    .then_inc(e_rowv, 1)

            def spread(m):
                return m.rearrange("p (o c) -> p o c", o=1)

            def set_flag():
                dve.wait_ge(ok_t, 1)
                tr(v.tensor_reduce(okm[0:1, 1:2], ps[0:1, 0, 256:256 + P], AX.X, ALU.min))
                v.tensor_scalar(flag[:, :], okm[0:1, 1:2], 0.5, None, ALU.is_lt).then_inc(flag_set, 1)

            def scores(s, n):
                t, h = KT * s + n // H, n % H
                if n % H == 0 and isinstance(s, int) and s == 0:
                    dve.wait_ge(*((pen_done, t + 1) if t < 2 else (pen_own, t - 1)))
                elif n % H == 0:
                    dve.wait_ge(pen_done, t - 1)
                if not (isinstance(s, int) and s == 0 and n < 2):
                    dve.wait_ge(den_done, KT * H * s + n - 1)
                hold(s)
                v.tensor_tensor_reduce(out=sc[:, n % 2, :], in0=pen[:, (n // H) % 2, :], in1=neb[:, h, :],
                                       scale=1.0, scalar=3.0e38, op0=ALU.add, op1=ALU.min,
                                       accum_out=negm[:, n:n + 1]).then_inc(sc_done, 1)

            def maximum(s, n):
                dve.wait_ge(sc_done, KT * H * s + n + 1)
                v.tensor_scalar(negmc[:, n:n + 1], negm[:, n:n + 1], -C, None, ALU.add).then_inc(max_done, 1)

            def logarithm_sum(s):
                dve.wait_ge(ln_done, s + 1)
                if not (isinstance(s, int) and s == 0):
                    dve.wait_ge(bc_done, H * s)
                v.tensor_tensor(nml[:, :], negm[:, :], den[:, :], ALU.subtract).then_inc(nml_done, 1)
                dve.wait_ge(nml_done, s + 1)

            def attend(b, j):
                dve.wait_ge(att_done, NT * b + j + 1)
                for h in range(H):
                    n = H * j + h
                    dve.wait_ge(t_done, H * NT * b + n + 1)
                    if not (isinstance(b, int) and b == 0 and n < UU):
                        dve.wait_ge(es_mm, H * NT * b + n - UU + 1)
                    v.tensor_tensor(uu[:, n % UU, :], tt[:, n % 4, :], att[:, j % 2, :],
                                    ALU.mult).then_inc(u_done, 1)

            def n_sum(f, c, bufs, bank):
                r, _, u, _ = bufs
                dve.wait_ge(g_part, 2 * GATE * f + GATE * c + 6)
                v.scalar_tensor_tensor(u, ps[:, bank[2], :], bi[:, 2 * c + 1, 2:3], r,
                                       ALU.add, ALU.mult).then_inc(g_dve, 1)
                dve.wait_ge(g_dve, 4 * f + 2 * c + 1)
                v.tensor_tensor(u, u, ps[:, bank[3], :], ALU.add).then_inc(g_dve, 1)

            def cell_out(f, c, bufs, to):
                _, z_, u, n_ = bufs
                own = chain(vg, OWN * f + CELL * c)
                own(v.tensor_tensor(u, h2t[:, bass.ts(f, BLK)], n_, ALU.subtract))
                own(v.tensor_tensor(u, z_, u, ALU.mult))
                own(v.tensor_tensor(to, u, n_, ALU.add))

            def block_out(f):
                dve.wait_ge(o_t, f + 1)
                dve.wait_ge(stored, 16 * f + 16)
                for k in range(KT):
                    last = v.scalar_tensor_tensor(osb[:, k:k + 1, :], ps[:, 7:8, k * D:(k + 1) * D],
                                                  de[:, bass.ds(KT * f + k, 1)],
                                                  xb[:, bass.ds(KT * f + k, 1), :], ALU.mult, ALU.add)
                last.then_inc(o_done, 1)

            def gru_step(f, j):
                if j in (6, 11):
                    c = j // 11
                    dve.wait_ge(g_act, 6 * f + 3 * c + 1)
                    n_sum(f, c, work[0], banks[0])
                if j in (8, 13):
                    c = j // 13
                    dve.wait_ge(g_act, 6 * f + 3 * c + 3)
                    cell_out(f, c, work[0], oe_ if c == 0 else uv_)
                if j == 13:
                    v.tensor_tensor(uv_, uv_, oe_, ALU.add).then_inc(o_sum, 1)
                if j == 15:
                    block_out(f)

            def layer1(b, first, last_):
                for j in range(NT):
                    if not last_ and j < KT * H:
                        scores(b + 1, j)
                    attend(b, j)
                    if not last_ and j < KT * H:
                        maximum(b + 1, j)
                    if not first:
                        gru_step(b - 1, j)
                    if not last_ and j == 14:
                        logarithm_sum(b + 1)

            def own_pen(t):
                dve.wait_ge(row_in[t % 2], 32)
                dve.wait_ge(sc_done, H * (t - 1))
                tr(v.tensor_scalar(pen[:, t % 2, :], row[:, t % 2, :], 0.0, OUT, ALU.is_le, ALU.mult))
                spot = pen[:, t % 2, P * t:P * t + P]
                v.tensor_tensor(spot, spot, outdiag[:, :], ALU.max).then_inc(pen_own, 1)

            for n in range(KT * H):
                if n < H:
                    copy_row(NB * n + 1)
                    copy_row(NB * n + 3)
                    dve.wait_ge(e_rowa, 2 * n + 2)
                    dve.wait_ge(e_rowv, 2 * n + 2)
                if n in (H, 2 * H):
                    own_pen(n // H + 1)
                scores(0, n)
                maximum(0, n)
                if n == H:
                    set_flag()
            logarithm_sum(0)
            layer1(0, True, False)
            with nc.vector.Fori(1, NB - 1) as b:
                layer1(b, False, False)
            layer1(NB - 1, False, True)
            f = NB - 1
            for c in range(2):
                dve.wait_ge(g_act, 6 * f + 3 * c + 1)
                n_sum(f, c, work_last[c], banks_last[c])
                dve.wait_ge(g_act, 6 * f + 3 * c + 3)
                cell_out(f, c, work_last[c], (oe_, work_last[1][2])[c])
            v.tensor_tensor(oe_, oe_, work_last[1][2], ALU.add).then_inc(o_sum, 1)
            block_out(f)

            def turn(at, steps, name):
                dve.wait_ge(general_step, at + steps.index(name))

            def done(ins):
                ins.then_inc(general_step, 1)

            def copies(at, steps, tag):
                for q in range(NB):
                    turn(at, steps, f"{tag} copy {q}")
                    done(v.tensor_copy(quad, ps[:, 0, :]))

            def normalise(at, steps):
                turn(at, steps, "stats")
                done(v.bn_stats(stat[:, 0, :], cur))
                turn(at, steps, "aggregate")
                hold(at)
                done(v.bn_aggr(mv[:, 0, :], stat[:, 0, :]))
                r, w_ = rstd[:, 0:1], nwt[:, 0:1]
                turn(at, steps, "newton 0")
                done(v.scalar_tensor_tensor(w_, mv[:, 0, 1:2], EPS, r, ALU.add, ALU.mult))
                turn(at, steps, "newton 1")
                done(v.tensor_tensor(w_, w_, r, ALU.mult))
                turn(at, steps, "newton 2")
                done(v.tensor_scalar(w_, w_, -0.5, 1.5, ALU.mult, ALU.add))
                turn(at, steps, "newton 3")
                done(v.tensor_tensor(r, r, w_, ALU.mult))
                turn(at, steps, "normalise")
                done(v.tensor_scalar(z, cur, mv[:, 0, 0:1], r, ALU.subtract, ALU.mult))
                turn(at, steps, "relu")
                done(v.tensor_scalar(z, z, 0.0, None, ALU.max))
                turn(at, steps, "copy z")
                done(v.tensor_copy(zt_g, ps[:, 0, 0:P]))

            def signs(at, steps, t):
                turn(at, steps, "no diagonal")
                spot = a_row[:, bass.ts(t, P)]
                done(v.tensor_tensor(spot, spot, offdiag[:, :], ALU.mult))
                turn(at, steps, "pos")
                done(v.tensor_scalar(pos, a_row, 0.0, None, ALU.is_gt))
                turn(at, steps, "neg")
                done(v.tensor_scalar(neg, a_row, 0.0, None, ALU.is_lt))

            signed = nc.vector.value_load(flag[0:1, 0:1], min_val=0, max_val=1)
            with nc.vector.If(signed != 0):
                dve.wait_ge(g_x_in, 16)
                with nc.vector.Fori(0, NT) as t:
                    at = len(MESSAGES) * t + S1
                    turn(at, MESSAGES, "fetch")
                    done(v.tensor_scalar(cur, xb[:, bass.ds(t, 1), :].rearrange("p o d -> p (o d)"),
                                         0.0, None, ALU.add))
                    normalise(at, MESSAGES)
                    turn(at, MESSAGES, "add b0")
                    done(v.tensor_tensor(g_msg[:, bass.ds(t, 1), :], ps[:, 1:2, 0:D],
                                         b0s[:, :].rearrange("p (o d) -> p o d", o=1), ALU.add))

                SMALL = 2.0 ** -40
                with nc.vector.Fori(0, NT) as t:
                    at = len(WEIGHTS) * t + S2
                    turn(at, WEIGHTS, "square")
                    dve.wait_ge(g_row_in, 16 * t + 16)
                    done(v.tensor_tensor(pos, a_row, a_row, ALU.mult))
                    turn(at, WEIGHTS, "clamp")
                    done(v.tensor_scalar(pos, pos, SMALL, None, ALU.max))
                    turn(at, WEIGHTS, "reciprocal")
                    done(v.reciprocal(neg, pos))
                    turn(at, WEIGHTS, "r")
                    done(v.tensor_tensor(neg, neg, a_row, ALU.mult))
                    turn(at, WEIGHTS, "q")
                    done(v.scalar_tensor_tensor(w_row, neg, -2.0, neg, ALU.add, ALU.mult))
                    turn(at, WEIGHTS, "below 1")
                    done(v.scalar_tensor_tensor(w_row, a_row, 1.0, w_row, ALU.is_lt, ALU.mult))
                    turn(at, WEIGHTS, "not 0")
                    done(v.scalar_tensor_tensor(w_row, pos, SMALL, w_row, ALU.is_gt, ALU.mult))
                    copies(at, WEIGHTS, "sum")
                    x_rows = xb[:, bass.ds(t, 1), :]
                    turn(at, WEIGHTS, "x1")
                    done(v.tensor_tensor(cur.rearrange("p (o d) -> p o d", o=1), ps[:, 1:2, 0:D],
                                         x_rows, ALU.add))
                    turn(at, WEIGHTS, "keep x1")
                    done(v.tensor_scalar(x_rows.rearrange("p o d -> p (o d)"), cur, 0.0, None, ALU.add))
                    normalise(at, WEIGHTS)
                    turn(at, WEIGHTS, "keep h2")
                    done(v.tensor_scalar(h2[:, bass.ds(t, 1), :].rearrange("p o d -> p (o d)"), z,
                                         0.0, None, ALU.add))
                    turn(at, WEIGHTS, "keep h2t")
                    done(v.tensor_scalar(h2t[:, bass.ts(t, P)], zt_g, 0.0, None, ALU.add))
                    turn(at, WEIGHTS, "keep hw")
                    done(v.tensor_scalar(hw[:, bass.ds(t, 1), :], ps[:, 1:2, 0:HWC], 0.0, None, ALU.add))

                with nc.vector.Fori(0, NT) as t:
                    at = len(NEIGHBOURS) * t + S3
                    dve.wait_ge(g_row_in, 16 * t + 16 * NT + 16)
                    signs(at, NEIGHBOURS, t)
                    copies(at, NEIGHBOURS, "plus")
                    copies(at, NEIGHBOURS, "minus")
                    turn(at, NEIGHBOURS, "keep plus")
                    done(v.tensor_copy(nbr, ps[:, 1, 0:2 * H]))
                    plus = nbr.rearrange("p (h s) -> p h s", s=2)
                    minus = ps[:, 2, 0:2 * H].rearrange("p (h s) -> p h s", s=2)
                    sums = g_sum[:, 0:2 * H]
                    turn(at, NEIGHBOURS, "e_plus")
                    done(v.tensor_tensor(sums[:, 0:H], plus[:, :, 0], minus[:, :, 1], ALU.add))
                    turn(at, NEIGHBOURS, "e_minus")
                    done(v.tensor_tensor(sums[:, H:2 * H], plus[:, :, 1], minus[:, :, 0], ALU.add))
                    for s, name in enumerate(("leaky plus", "leaky minus")):
                        turn(at, NEIGHBOURS, name)
                        part_ = sums[:, H * s:H * s + H].rearrange("p (h o) -> p h o", o=1)
                        done(v.scalar_tensor_tensor(e_col[:, H * s:H * s + H, bass.ds(t, 1)], part_, 0.2,
                                                    part_, ALU.mult, ALU.max))

                with nc.vector.Fori(0, NT) as t:
                    at = len(SPREAD) * t + S4
                    turn(at, SPREAD, "diagonals")
                    done(v.tensor_tensor(dg6, spread(ident[:, :]).broadcast_to([P, 2 * H, P]),
                                         e_col[:, :, bass.ds(t, 1)].broadcast_to([P, 2 * H, P]), ALU.mult))
                    for s, name in enumerate(("copy plus", "copy minus")):
                        turn(at, SPREAD, name)
                        done(v.tensor_scalar(e_all[:, H * s:H * s + H, bass.ts(t, P)],
                                             ps[:, 1 + s, 0:H * P].rearrange("p (h c) -> p h c", h=H),
                                             0.0, None, ALU.add))

                with nc.vector.Fori(0, NT) as t:
                    at = len(ATTEND) * t + S5
                    dve.wait_ge(g_row_in, 16 * t + 32 * NT + 16)
                    signs(at, ATTEND, t)
                    turn(at, ATTEND, "none")
                    done(v.tensor_scalar(none, a_row, 0.0, -9.0e15, ALU.is_equal, ALU.mult))
                    copies(at, ATTEND, "node")
                    for h in range(H):
                        def head(name):
                            turn(at, ATTEND, f"{h} {name}")

                        head("plus score")
                        done(v.tensor_tensor(score, pos, e_all[:, h, :], ALU.mult))
                        head("minus score")
                        done(v.tensor_tensor(score2, neg, e_all[:, H + h, :], ALU.mult))
                        head("both")
                        done(v.tensor_tensor(score, score, score2, ALU.add))
                        head("outside")
                        done(v.tensor_tensor(score, score, none, ALU.add))
                        head("max")
                        done(v.tensor_reduce(g_small[:, G_MAX:G_MAX + 1], score, AX.X, ALU.max))
                        head("bias")
                        done(v.tensor_scalar(g_small[:, G_BIAS:G_BIAS + 1], g_small[:, G_MAX:G_MAX + 1],
                                             -1.0, -C, ALU.mult, ALU.add))
                        head("denominator")
                        done(v.tensor_reduce(g_small[:, G_DEN:G_DEN + 1], score, AX.X, ALU.add))
                        head("reciprocal")
                        done(v.reciprocal(g_small[:, G_RDEN:G_RDEN + 1], g_small[:, G_DEN:G_DEN + 1]))
                        head("probability")
                        done(v.scalar_tensor_tensor(w_row, score, g_small[:, G_RDEN:G_RDEN + 1], a_row,
                                                    ALU.mult, ALU.mult))
                        copies(at, ATTEND, f"{h} edge")
                    for s, name in enumerate(("keep node", "keep edge")):
                        turn(at, ATTEND, name)
                        done(v.tensor_scalar(sup_rows[:, s, :], ps[:, 1 + s, 0:D], (1.0, 1.0 / H)[s], None,
                                             ALU.mult))
                    turn(at, ATTEND, "copy supports")
                    done(v.tensor_copy(sup2, ps[:, 0, 0:2 * P].rearrange("p (s c) -> p s c", s=2)))
                    for c in range(2):
                        def cell(name):
                            turn(at, ATTEND, f"{c} {name}")

                        cell("times r")
                        done(v.scalar_tensor_tensor(g_r, ps[:, 5, 0:P], bi[:, 2 * c + 1, 2:3], g_r,
                                                    ALU.add, ALU.mult))
                        cell("add in")
                        done(v.tensor_tensor(g_r, g_r, ps[:, 6, 0:P], ALU.add))
                        cell("h - n")
                        done(v.tensor_tensor(g_d, h2t[:, bass.ts(t, P)], g_n, ALU.subtract))
                        cell("times z")
                        done(v.tensor_tensor(g_d, g_d, g_z, ALU.mult))
                        cell("add n")
                        done(v.tensor_tensor(g_out if c == 0 else g_sum, g_d, g_n, ALU.add))
                    turn(at, ATTEND, "add cells")
                    done(v.tensor_tensor(g_sum, g_sum, g_out, ALU.add))
                    turn(at, ATTEND, "out")
                    done(v.scalar_tensor_tensor(g_out.rearrange("p (o d) -> p o d", o=1), ps[:, 0:1, 0:P],
                                                de[:, bass.ds(t, 1)], xb[:, bass.ds(t, 1), :],
                                                ALU.mult, ALU.add))


_INS = ["x", "adj", "L0_gnn_W", "L0_gnn_B", "L1_gnn_gat_W", "L1_gnn_gat_a",
        "L1_gnn_edge_Wih", "L1_gnn_edge_Whh", "L1_gnn_edge_bih", "L1_gnn_edge_bhh",
        "L1_gnn_node_Wih", "L1_gnn_node_Whh", "L1_gnn_node_bih", "L1_gnn_node_bhh"]


def kernel(**inputs):
    import concourse.bacc as _bacc
    from concourse.bass_utils import run_bass_kernel_spmd as _run

    nc = _bacc.Bacc("TRN2", target_bir_lowering=False, num_devices=1)
    arrays, args = {}, []
    for name in _INS:
        a = np.ascontiguousarray(inputs[name])
        arrays[f"in_{name}"] = a
        args.append(nc.dram_tensor(f"in_{name}", a.shape, mybir.dt.from_np(a.dtype), kind="ExternalInput").ap())
    args.append(nc.dram_tensor("out_x", (N, D), F32, kind="ExternalOutput").ap())
    program(nc, *args)
    r = _run(nc, [arrays], core_ids=[0])
    return r.results[0]["out_x"]
```
